# Optimizing a Trainium2 kernel written in Bass

```python
import numpy as np
import jax
import jax.numpy as jnp

def _softmax(x, axis=-1):
    return jax.nn.softmax(x, axis=axis)

def _gelu(x):
    return jax.nn.gelu(x, approximate=True)

def _silu(x):
    return jax.nn.silu(x)

def _sigmoid(x):
    return jax.nn.sigmoid(x)

def _layernorm(x, axis=-1, eps=1e-05):
    m = jnp.mean(x, axis=axis, keepdims=True)
    v = jnp.var(x, axis=axis, keepdims=True)
    return (x - m) / jnp.sqrt(v + eps)

def _scatter_add(tgt, idx, src, axis=0):
    return tgt.at[idx].add(src)

def _segment_sum(src, seg, n):
    return jax.ops.segment_sum(src, seg, n)
kernel_name = 'mk_macaron_d1_jaxref_r2_626f07'

def setup_inputs(seed: int=0):
    np.random.seed(seed)
    _w = jnp.asarray

    def _L0_attn_setup():
        import jax, jax.numpy as jnp
        import numpy as np
        B, T, D, W = (2, 4096, 1024, 128)
        PAD = -1.0
        key = jax.random.key(seed)
        k1, k2, k3 = jax.random.split(key, 3)
        x = jax.random.normal(k1, (B, T, D), jnp.float32)
        w_attn = jax.random.normal(k2, (3 * D, D), jnp.float32) * 0.02
        w_o = jax.random.normal(k3, (D, D), jnp.float32) * 0.02
        return {'x': x, 'w_attn': w_attn, 'w_o': w_o}
    _L0_attn_in = _L0_attn_setup()

    def _L0_ffn_setup():
        import jax, jax.numpy as jnp
        import numpy as np
        EPS = 1e-06
        K_STEPS = 4
        USE_GATING = True

        def layer_norm(x, gamma, beta):
            mu = jnp.mean(x, axis=-1, keepdims=True)
            var = jnp.mean(jnp.square(x - mu), axis=-1, keepdims=True)
            return (x - mu) * jax.lax.rsqrt(var + EPS) * gamma + beta
        key = jax.random.key(seed)
        B, L, D, H = (4, 2048, 1024, 4096)
        ks = jax.random.split(key, 16)
        s = 0.02
        return {'x': jax.random.normal(ks[0], (B, L, D), dtype=jnp.float32), 'in_gamma': jnp.ones((D,), jnp.float32), 'in_beta': jnp.zeros((D,), jnp.float32), 'agg_w': jax.random.normal(ks[1], (D, D), jnp.float32) * s, 'agg_b': jnp.zeros((D,), jnp.float32), 'pn_gamma': jnp.ones((D,), jnp.float32), 'pn_beta': jnp.zeros((D,), jnp.float32), 'd1_w': jax.random.normal(ks[2], (D, H), jnp.float32) * s, 'd1_b': jnp.zeros((H,), jnp.float32), 'd2_w': jax.random.normal(ks[3], (H, D), jnp.float32) * s, 'd2_b': jnp.zeros((D,), jnp.float32), 'bc_w': jax.random.normal(ks[4], (D, D), jnp.float32) * s, 'bc_b': jnp.zeros((D,), jnp.float32), 'gate_w': jax.random.normal(ks[5], (D, D), jnp.float32) * s, 'gate_b': jnp.zeros((D,), jnp.float32), 'out_gamma': jnp.ones((D,), jnp.float32), 'out_beta': jnp.zeros((D,), jnp.float32)}
    _L0_ffn_in = _L0_ffn_setup()
    _d = {'L0_attn_x': _L0_attn_in['x'], 'L0_attn_w_attn': _L0_attn_in['w_attn'], 'L0_attn_w_o': _L0_attn_in['w_o'], 'L0_ffn_in_gamma': _L0_ffn_in['in_gamma'], 'L0_ffn_in_beta': _L0_ffn_in['in_beta'], 'L0_ffn_agg_w': _L0_ffn_in['agg_w'], 'L0_ffn_agg_b': _L0_ffn_in['agg_b'], 'L0_ffn_pn_gamma': _L0_ffn_in['pn_gamma'], 'L0_ffn_pn_beta': _L0_ffn_in['pn_beta'], 'L0_ffn_d1_w': _L0_ffn_in['d1_w'], 'L0_ffn_d1_b': _L0_ffn_in['d1_b'], 'L0_ffn_d2_w': _L0_ffn_in['d2_w'], 'L0_ffn_d2_b': _L0_ffn_in['d2_b'], 'L0_ffn_bc_w': _L0_ffn_in['bc_w'], 'L0_ffn_bc_b': _L0_ffn_in['bc_b'], 'L0_ffn_gate_w': _L0_ffn_in['gate_w'], 'L0_ffn_gate_b': _L0_ffn_in['gate_b'], 'L0_ffn_out_gamma': _L0_ffn_in['out_gamma'], 'L0_ffn_out_beta': _L0_ffn_in['out_beta']}
    _x0 = _d['L0_attn_x']
    _d['L0_attn_x'] = jax.random.normal(jax.random.fold_in(jax.random.key(seed), 1), (2, 2048, 1024), dtype=_x0.dtype)
    del _x0
    return _d

def reference(L0_attn_x, L0_attn_w_attn, L0_attn_w_o, L0_ffn_in_gamma, L0_ffn_in_beta, L0_ffn_agg_w, L0_ffn_agg_b, L0_ffn_pn_gamma, L0_ffn_pn_beta, L0_ffn_d1_w, L0_ffn_d1_b, L0_ffn_d2_w, L0_ffn_d2_b, L0_ffn_bc_w, L0_ffn_bc_b, L0_ffn_gate_w, L0_ffn_gate_b, L0_ffn_out_gamma, L0_ffn_out_beta):

    def _L0_attn_ref(x, w_attn, w_o):
        import jax, jax.numpy as jnp
        import numpy as np
        B, T, D, W = (2, 4096, 1024, 128)
        PAD = -1.0
        Bn, Tn, Dn = x.shape
        w = Tn // W
        qkv = x @ w_attn.T
        q, k, v = jnp.split(qkv, 3, axis=-1)
        q = q / W
        bq = q.reshape(Bn, w, W, Dn)
        bk = k.reshape(Bn, w, W, Dn)
        bv = v.reshape(Bn, w, W, Dn)
        pad_blk = jnp.full((Bn, 1, W, Dn), PAD, dtype=x.dtype)
        bk_prev = jnp.concatenate([pad_blk, bk[:, :-1]], axis=1)
        bv_prev = jnp.concatenate([pad_blk, bv[:, :-1]], axis=1)
        bk2 = jnp.concatenate([bk_prev, bk], axis=2)
        bv2 = jnp.concatenate([bv_prev, bv], axis=2)
        t = jnp.arange(Tn, dtype=jnp.int32).reshape(w, W)
        t_prev = jnp.concatenate([jnp.full((1, W), -1, jnp.int32), t[:-1]], axis=0)
        tj = jnp.concatenate([t_prev, t], axis=1)
        ti = t[:, :, None]
        tjb = tj[:, None, :]
        keep = (ti >= tjb) & (ti <= tjb + W) & (tjb != -1)
        sim = jnp.einsum('bwie,bwje->bwij', bq, bk2)
        sim = jnp.where(keep[None], sim, 0.0)
        attn = jnp.square(jax.nn.relu(sim))
        out = jnp.einsum('bwij,bwje->bwie', attn, bv2)
        out = out.reshape(Bn, Tn, Dn)
        return out @ w_o.T

    def _L0_ffn_ref(x, in_gamma, in_beta, agg_w, agg_b, pn_gamma, pn_beta, d1_w, d1_b, d2_w, d2_b, bc_w, bc_b, gate_w, gate_b, out_gamma, out_beta):
        import jax, jax.numpy as jnp
        import numpy as np
        EPS = 1e-06
        K_STEPS = 4
        USE_GATING = True

        def layer_norm(x, gamma, beta):
            mu = jnp.mean(x, axis=-1, keepdims=True)
            var = jnp.mean(jnp.square(x - mu), axis=-1, keepdims=True)
            return (x - mu) * jax.lax.rsqrt(var + EPS) * gamma + beta
        x_norm = layer_norm(x, in_gamma, in_beta)
        thought = x_norm[:, -1, :] @ agg_w + agg_b
        for _ in range(K_STEPS):
            t = layer_norm(thought, pn_gamma, pn_beta)
            t = jax.nn.gelu(t @ d1_w + d1_b, approximate=False)
            thought = thought + (t @ d2_w + d2_b)
        broadcast = (thought @ bc_w + bc_b)[:, None, :]
        if USE_GATING:
            gate = jax.nn.sigmoid(x @ gate_w + gate_b)
            out = x + gate * broadcast
        else:
            out = x + broadcast
        return layer_norm(out, out_gamma, out_beta)
    x = L0_attn_x
    x = x + 0.5 * _L0_ffn_ref(_layernorm(x, axis=-1), L0_ffn_in_gamma, L0_ffn_in_beta, L0_ffn_agg_w, L0_ffn_agg_b, L0_ffn_pn_gamma, L0_ffn_pn_beta, L0_ffn_d1_w, L0_ffn_d1_b, L0_ffn_d2_w, L0_ffn_d2_b, L0_ffn_bc_w, L0_ffn_bc_b, L0_ffn_gate_w, L0_ffn_gate_b, L0_ffn_out_gamma, L0_ffn_out_beta)
    x = x + _L0_attn_ref(_layernorm(x, axis=-1), L0_attn_w_attn, L0_attn_w_o)
    x = x + 0.5 * _L0_ffn_ref(_layernorm(x, axis=-1), L0_ffn_in_gamma, L0_ffn_in_beta, L0_ffn_agg_w, L0_ffn_agg_b, L0_ffn_pn_gamma, L0_ffn_pn_beta, L0_ffn_d1_w, L0_ffn_d1_b, L0_ffn_d2_w, L0_ffn_d2_b, L0_ffn_bc_w, L0_ffn_bc_b, L0_ffn_gate_w, L0_ffn_gate_b, L0_ffn_out_gamma, L0_ffn_out_beta)
    return x

_drawn_inputs = setup_inputs


def setup_inputs(seed=0):
    import zlib

    import numpy as np

    out = dict(_drawn_inputs(seed))
    spreads = {'L0_ffn_in_gamma': (1.0, 0.2),
     'L0_ffn_in_beta': (0.0, 0.1),
     'L0_ffn_agg_b': (0.0, 0.1),
     'L0_ffn_pn_gamma': (1.0, 0.2),
     'L0_ffn_pn_beta': (0.0, 0.1),
     'L0_ffn_d1_b': (0.0, 0.1),
     'L0_ffn_d2_b': (0.0, 0.1),
     'L0_ffn_bc_b': (0.0, 0.308),
     'L0_ffn_gate_b': (0.0, 0.563),
     'L0_ffn_out_gamma': (1.0, 0.2),
     'L0_ffn_out_beta': (0.0, 0.1)}
    factors = {}
    for name, (base, spread) in spreads.items():
        noise = np.random.default_rng([zlib.crc32(name.encode()), seed]).standard_normal(out[name].shape)
        drawn = base * np.exp(spread * noise) if base else spread * noise
        out[name] = jnp.asarray(drawn.astype(out[name].dtype))
    for name, factor in factors.items():
        out[name] = (out[name] * factor).astype(out[name].dtype)
    return out
```

```python
from contextlib import ExitStack

import concourse.bass as bass
from concourse import mybir

F32 = mybir.dt.float32
F16 = mybir.dt.float16
I32 = mybir.dt.int32
ALU = mybir.AluOpType
ACT = mybir.ActivationFunctionType
AX_X = mybir.AxisListType.X

P = 128
BANK = 512
PE_COLS = 32
K_STEPS = 4
EPS_OUTER = 1e-5
EPS_FFN = 1e-6
TOKEN_SCALE = 1024.0
EXPONENT_BITS = 0x7F800000
WEIGHT_TOP = 8192.0
TINY = 2.0 ** -100
NEVER = 3.0e38


class Ticket:

    def __init__(self, sem, value):
        self.sem, self.value = sem, value


class Stream:

    def __init__(self, eng, sem, serial):
        self.eng, self.sem, self.count, self.serial, self.seen = eng, sem, 0, serial, {}

    def wait(self, *tickets):
        for t in tickets:
            if isinstance(t, (list, tuple)):
                self.wait(*t)
            elif t is not None and self.seen.get(t.sem.name, 0) < t.value:
                self.eng.wait_ge(t.sem, t.value)
                self.seen[t.sem.name] = t.value

    def done(self, instruction):
        instruction.then_inc(self.sem, 1)
        self.count += 1
        t = Ticket(self.sem, self.count)
        if self.serial:
            self.wait(t)
        return t

    def last(self):
        return Ticket(self.sem, self.count) if self.count else None


class Buffer:

    def __init__(self, ap, dma_sem=None):
        self.ap, self.dma_sem, self.dma_count = ap, dma_sem, 0
        self.ready, self.free = [], []


class Ring:
    def __init__(self, buffers):
        self.buffers, self.at = buffers, 0

    def take(self):
        self.at += 1
        return self.buffers[(self.at - 1) % len(self.buffers)]


class Shelf:

    def __init__(self, buffers):
        self.free = list(buffers)

    def take(self):
        return self.free.pop(0)

    def give(self, *buffers):
        self.free.extend(buffers)


def macaron_kernel(nc, x, w_attn, w_o, in_gamma, in_beta, agg_w, agg_b, pn_gamma, pn_beta,
                   d1_w, d1_b, d2_w, d2_b, bc_w, bc_b, gate_w, gate_b, out_gamma, out_beta, out):
    B, T, D = x.shape
    H = d1_w.shape[1]
    KD, KH = D // P, H // P
    NT = T // P
    HALVES = D // BANK
    GROUP = 2
    WCHUNK = 2 * D
    assert B == 2 and D == 1024 and H % WCHUNK == 0 and NT % GROUP == 0

    x_flat, out_flat = (a.rearrange("b t d -> (b t) d") for a in (x, out))
    row_of = lambda tile: slice(tile * P, (tile + 1) * P)
    gate1_dram = nc.dram_tensor("gate1_scratch", [B * T, D], F32, kind="Internal").ap()
    x1_dram = nc.dram_tensor("x1_scratch", [B * T, D], F32, kind="Internal").ap()
    x2_dram = nc.dram_tensor("x2_scratch", [B * T, D], F32, kind="Internal").ap()
    qk_dram = nc.dram_tensor("qk_scratch", [D, D], F32, kind="Internal").ap()
    vo_dram = nc.dram_tensor("vo_scratch", [D, D], F32, kind="Internal").ap()
    row_dram = nc.dram_tensor("row_scratch", [B * KD, P], F32, kind="Internal").ap()

    whole = ExitStack()
    with whole:
        every_dma = []

        def new_sem(name):
            return whole.enter_context(nc.semaphore(name))

        pe = Stream(nc.tensor, new_sem("pe_done"), serial=False)
        act = Stream(nc.scalar, new_sem("act_done"), serial=True)
        dve = Stream(nc.vector, new_sem("dve_done"), serial=True)
        pool = Stream(nc.gpsimd, new_sem("pool_done"), serial=True)
        sp = Stream(nc.sync, new_sem("sp_done"), serial=False)
        engines = (pe, act, dve, pool, sp)

        def sbuf(stack, name, shape, dtype=F32):
            return stack.enter_context(nc.sbuf_tensor(name, shape, dtype))

        dma_sems = {}

        def dma_sem(name):
            if name not in dma_sems:
                dma_sems[name] = [new_sem(name), 0]
            return dma_sems[name]

        def dma(to, source, sem, *waits):
            sp.wait(*waits)
            nc.sync.dma_start(to, source).then_inc(sem[0], 16)
            sem[1] += 16
            return Ticket(sem[0], sem[1])

        def buffers(stack, name, n, shape, dtype=F32):
            return [Buffer(sbuf(stack, f"{name}{i}", shape, dtype), dma_sem(f"dma_{name}{i}"))
                    for i in range(n)]

        def ring(stack, name, n, shape, dtype=F32):
            return Ring(buffers(stack, name, n, shape, dtype))

        def load(buf, to, source, *waits):
            buf.ready = [dma(to, source, buf.dma_sem, buf.free, *waits)]
            buf.free = []

        def store(buf, to, source):
            t = dma(to, source, buf.dma_sem, buf.ready)
            buf.free.append(t)
            return t

        def join():
            tickets = [e.last() for e in engines]
            tickets += [Ticket(s, n) for s, n in dma_sems.values() if n]
            for e in engines:
                e.wait(*tickets)

        product_banks = whole.enter_context(nc.psum_tensor("product_banks", [P, 4, BANK], F32))
        turn_banks = whole.enter_context(nc.psum_tensor("turn_banks", [P, 2, BANK], F32))
        thought_acc = Buffer(whole.enter_context(nc.psum_tensor("thought_acc", [P, BANK], F32))[:, :])
        thought_turn = Buffer(whole.enter_context(nc.psum_tensor("thought_turn", [P, BANK], F32))[:, :])
        product_ring = Ring([Buffer(product_banks[:, i, :]) for i in range(4)])
        turn_ring = Ring([Buffer(turn_banks[:, i, :]) for i in range(2)])

        identity = sbuf(whole, "identity", [P, P])
        mean_maker = sbuf(whole, "mean_maker", [P, P])
        keep_prev = sbuf(whole, "keep_prev", [P, P])
        keep_own = sbuf(whole, "keep_own", [P, P])
        minus_half = sbuf(whole, "minus_half", [P, 2])
        half_gamma = sbuf(whole, "half_gamma", [P, D])
        half_beta = sbuf(whole, "half_beta", [P, D])
        thought_row = Buffer(sbuf(whole, "thought_row", [P, B, D]), dma_sem("dma_thought_row"))
        token_stats = sbuf(whole, "token_stats", [P, B * NT, 2])
        bn_parts = sbuf(whole, "bn_parts", [P, HALVES, 6])
        bn_out = sbuf(whole, "bn_out", [P, 4])
        weight_ring = ring(whole, "thought_weights", 3, [P, WCHUNK])
        wide_a = Buffer(sbuf(whole, "wide_a", [P, KD, D]), dma_sem("dma_wide_a"))
        wide_b = Buffer(sbuf(whole, "wide_b", [P, KD, D]), dma_sem("dma_wide_b"))
        thought = sbuf(whole, "thought", [P, B, KD])
        centred = sbuf(whole, "centred", [P, B, KD])
        squares = sbuf(whole, "squares", [P, B, KD])
        t_small = sbuf(whole, "t_small", [P, 3, B])
        hidden = sbuf(whole, "hidden", [P, B, KH])
        t_rows = sbuf(whole, "t_rows", [P, P])
        t_pad = sbuf(whole, "t_pad", [P, P])
        narrow_in = sbuf(whole, "narrow_in", [P, KD, B])
        narrow_hidden = sbuf(whole, "narrow_hidden", [P, KH, B])
        t_wide = Buffer(sbuf(whole, "t_wide", [P, BANK]))
        vectors = sbuf(whole, "vectors", [P, P])
        d1_bias = sbuf(whole, "d1_bias", [P, KH])
        scale_stat = sbuf(whole, "scale_stat", [P, KD + 4])
        inverse = {m: sbuf(whole, f"inverse_{m}", [P, 1]) for m in ("gate", "qk", "vo")}

        pool.done(nc.gpsimd.memset(identity[:, :], 0.0))
        pool.done(nc.gpsimd.affine_select(out=identity[:, :], in_=identity[:, :], compare_op=ALU.not_equal,
                                          fill=1.0, base=0, pattern=[[-1, P]], channel_multiplier=1))
        for keep in (keep_prev, keep_own):
            pool.done(nc.gpsimd.memset(keep[:, :], NEVER))
        pool.done(nc.gpsimd.affine_select(out=keep_prev[:, :], in_=keep_prev[:, :], compare_op=ALU.is_ge,
                                          fill=0.0, base=0, pattern=[[-1, P]], channel_multiplier=1))
        constants = pool.done(nc.gpsimd.affine_select(
            out=keep_own[:, :], in_=keep_own[:, :], compare_op=ALU.is_ge,
            fill=0.0, base=0, pattern=[[1, P]], channel_multiplier=-1))
        dve.done(nc.vector.memset(mean_maker[:, :], 1.0 / D))
        dve.done(nc.vector.memset(minus_half[:, :], -0.5))
        dve.done(nc.vector.memset(thought_acc.ap, 0.0))
        dve.done(nc.vector.memset(t_pad[:, :], 0.0))
        zeroed = dve.done(nc.vector.memset(t_rows[:, :], 0.0))
        pe.wait(constants, zeroed)

        dma(half_gamma[:, :], out_gamma.partition_broadcast(P), dma_sem("dma_params"))
        params = dma(half_beta[:, :], out_beta.partition_broadcast(P), dma_sem("dma_params"))
        dve.wait(params)
        dve.done(nc.vector.tensor_scalar(half_gamma[:, :], half_gamma[:, :], 0.5, None, ALU.mult))
        scaled_params = dve.done(nc.vector.tensor_scalar(half_beta[:, :], half_beta[:, :], 0.5, None, ALU.mult))
        pool.wait(scaled_params)

        def turn_rows(rows_ready, dest, n):
            pe.wait(rows_ready, thought_turn.free)
            t = pe.done(nc.tensor.transpose(thought_turn.ap[:, 0:P], t_rows[:, :], identity[:, :]))
            dve.wait(t)
            t = dve.done(nc.vector.tensor_copy(dest, thought_turn.ap[:, 0:n]))
            thought_turn.free = [t]
            return t

        names = (in_gamma, in_beta, agg_b, pn_gamma, pn_beta, d2_b, bc_b)
        sp.wait(zeroed)
        for v, vec in enumerate(names):
            for b in range(B):
                at = (v * B + b) * KD
                rows = dma(t_rows[at:at + KD, :], vec.rearrange("(k p) -> k p", p=P),
                           dma_sem("dma_vectors"))
        turned = turn_rows(rows, vectors[:, 0:len(names) * B * KD], len(names) * B * KD)
        rows = dma(t_rows[0:KH, :], d1_b.rearrange("(k p) -> k p", p=P), dma_sem("dma_d1_bias"), turned)
        t_rows_free = turn_rows(rows, d1_bias[:, :], KH)
        V_IN_G, V_IN_B, V_AGG_B, V_PN_G, V_PN_B, V_D2_B, V_BC_B = range(len(names))
        vector_of = lambda v, b: vectors[:, (v * B + b) * KD:(v * B + b + 1) * KD]

        def weight_blocks():
            def narrow(w, tiles):
                for k in range(0, tiles, 2):
                    yield w[k * P:(k + 2) * P, :].rearrange("(k p) n -> p k n", p=P)

            def wide(w):
                for c in range(H // WCHUNK):
                    for k in range(KD):
                        yield w[k * P:(k + 1) * P, c * WCHUNK:(c + 1) * WCHUNK]

            for _ in range(2):
                yield from narrow(agg_w, KD)
                for _ in range(K_STEPS):
                    yield from wide(d1_w)
                    yield from narrow(d2_w, KH)
                yield from narrow(bc_w, KD)

        blocks = weight_blocks()
        pending = []

        def fetch_block():
            source = next(blocks, None)
            if source is not None:
                buf = weight_ring.take()
                to = buf.ap[:, :]
                if len(source.shape) == 3:
                    to = to.rearrange("p (k n) -> p k n", k=2)
                load(buf, to, source)
                pending.append(buf)

        def next_block():
            return pending.pop(0)

        def used_block(buf, t):
            buf.free = [t]
            fetch_block()

        def norm_thought(source, dest, eps, ready, gamma=None, beta=None):
            pe.wait(ready, thought_turn.free)
            t = pe.done(nc.tensor.matmul(thought_turn.ap[:, 0:B * KD], mean_maker[:, :],
                                         source[:, :, :].rearrange("p b k -> p (b k)"), start=True, stop=True))
            sums = thought_turn.ap[:, 0:B * KD].rearrange("p (b k) -> p b k", b=B)
            dve.wait(t)
            dve.done(nc.vector.tensor_reduce(t_small[:, 0, :], sums, AX_X, ALU.add))
            for b in range(B):
                dve.done(nc.vector.tensor_scalar(centred[:, b, :], source[:, b, :], t_small[:, 0, b:b + 1],
                                                 None, ALU.subtract))
            t = dve.done(nc.vector.tensor_tensor(squares[:, :, :], centred[:, :, :], centred[:, :, :], ALU.mult))
            yield
            pe.wait(t)
            t = pe.done(nc.tensor.matmul(thought_turn.ap[:, 0:B * KD], mean_maker[:, :],
                                         squares[:, :, :].rearrange("p b k -> p (b k)"), start=True, stop=True))
            dve.wait(t)
            t = dve.done(nc.vector.tensor_reduce(t_small[:, 1, :], sums, AX_X, ALU.add))
            thought_turn.free = [t]
            t = dve.done(nc.vector.tensor_scalar(t_small[:, 1, :], t_small[:, 1, :], eps, None, ALU.add))
            pool.wait(t)
            t = pool.done(nc.gpsimd.tensor_tensor(t_small[:, 2, :], t_small[:, 1, :], minus_half[:, 0:B], ALU.pow))
            dve.wait(t)
            for b in range(B):
                scaled = centred[:, b, :] if gamma is not None else dest(b)
                if gamma is None:
                    t = dve.done(nc.vector.tensor_scalar(dest(b), centred[:, b, :], t_small[:, 2, b:b + 1],
                                                         None, ALU.mult))
                else:
                    dve.done(nc.vector.scalar_tensor_tensor(
                        out=scaled, in0=centred[:, b, :], scalar=t_small[:, 2, b:b + 1],
                        in1=vector_of(gamma, b), op0=ALU.mult, op1=ALU.mult))
                    t = dve.done(nc.vector.tensor_tensor(dest(b), scaled, vector_of(beta, b), ALU.add))
            yield t

        def turn_sums(t):
            dve.wait(t, t_wide.free)
            t = dve.done(nc.vector.tensor_copy(t_wide.ap[:, :], thought_acc.ap[:, :]))
            thought_acc.free = [t]
            yield
            pe.wait(t, thought_turn.free)
            for s in range(BANK // P):
                mm = nc.tensor.transpose(thought_turn.ap[:, s * P:(s + 1) * P],
                                         t_wide.ap[:, s * P:(s + 1) * P], identity[:, :])
            t = pe.done(mm)
            t_wide.free = [t]
            yield t

        def turned_view(j, b):
            return thought_turn.ap.rearrange("p (s r) -> p s r", r=P)[:, :, PE_COLS * j + b]

        def narrow_product(stationary, tiles, ready, finish):
            pe.wait(ready, thought_acc.free)
            for i in range(0, tiles, 2):
                buf = next_block()
                pe.wait(buf.ready)
                w = buf.ap[:, :].rearrange("p (k n) -> p k n", k=2)
                for a in range(2):
                    for h in range(HALVES):
                        j = 2 * a + h
                        mm = nc.tensor.matmul(thought_acc.ap[PE_COLS * j:PE_COLS * j + B, :],
                                              stationary[:, i + a, :], w[:, a, h * BANK:(h + 1) * BANK],
                                              start=(i == 0), stop=(i == tiles - 2))
                t = pe.done(mm)
                used_block(buf, t)
                yield
            for t in turn_sums(t):
                yield
            dve.wait(t)
            per = BANK // P
            for b in range(B):
                for h in range(HALVES):
                    both = thought_turn.ap.rearrange("p (s a r) -> p s a r", a=2, r=2 * PE_COLS)[
                        :, :, :, PE_COLS * h + b]
                    t = dve.done(nc.vector.tensor_reduce(squares[:, b, h * per:(h + 1) * per], both, AX_X, ALU.add))
            thought_turn.free = [t]
            finish()

        def add_bias(bias, dest):
            def go():
                for b in range(B):
                    dve.done(nc.vector.tensor_tensor(dest[:, b, :], squares[:, b, :], vector_of(bias, b), ALU.add))
            return go

        def add_step():
            add_bias(V_D2_B, squares)()
            dve.done(nc.vector.tensor_tensor(thought[:, :, :], thought[:, :, :], squares[:, :, :], ALU.add))

        def wide_product(ready):
            for c in range(H // WCHUNK):
                pe.wait(ready, thought_acc.free)
                for k in range(KD):
                    buf = next_block()
                    pe.wait(buf.ready)
                    for j in range(WCHUNK // BANK):
                        mm = nc.tensor.matmul(thought_acc.ap[PE_COLS * j:PE_COLS * j + B, :],
                                              narrow_in[:, k, :], buf.ap[:, j * BANK:(j + 1) * BANK],
                                              start=(k == 0), stop=(k == KD - 1))
                    t = pe.done(mm)
                    used_block(buf, t)
                    yield
                for t in turn_sums(t):
                    yield
                dve.wait(t)
                per = BANK // P
                for b in range(B):
                    for j in range(WCHUNK // BANK):
                        at = (c * (WCHUNK // BANK) + j) * per
                        t = dve.done(nc.vector.tensor_tensor(hidden[:, b, at:at + per], turned_view(j, b),
                                                             d1_bias[:, at:at + per], ALU.add))
                thought_turn.free = [t]
            act.wait(t, pe.last())
            for b in range(B):
                t = act.done(nc.scalar.activation(narrow_hidden[:, :, b], hidden[:, b, :], ACT.Gelu))
            yield t

        def think(source_rows, ready):
            nonlocal t_rows_free
            for b in range(B):
                rows = dma(t_rows[b * KD:(b + 1) * KD, :], source_rows(b), dma_sem("dma_thought_in"),
                           ready, t_rows_free)
            t = t_rows_free = turn_rows(rows, thought[:, :, :].rearrange("p b k -> p (b k)"), B * KD)
            yield
            into_thought = lambda b: thought[:, b, :]
            into_narrow = lambda b: narrow_in[:, :, b]
            for t in norm_thought(thought, into_thought, EPS_OUTER, t):
                yield
            for t in norm_thought(thought, into_narrow, EPS_FFN, t, V_IN_G, V_IN_B):
                yield
            yield from narrow_product(narrow_in, KD, t, add_bias(V_AGG_B, thought))
            for _ in range(K_STEPS):
                for t in norm_thought(thought, into_narrow, EPS_FFN, dve.last(), V_PN_G, V_PN_B):
                    yield
                for t in wide_product(t):
                    yield
                yield from narrow_product(narrow_hidden, KH, t, add_step)
            for b in range(B):
                t = dve.done(nc.vector.tensor_copy(narrow_in[:, :, b], thought[:, b, :]))
            yield from narrow_product(narrow_in, KD, t, add_bias(V_BC_B, t_pad[:, 0:B * KD].rearrange(
                "p (b k) -> p b k", b=B)))
            pe.wait(dve.last(), thought_turn.free)
            t = pe.done(nc.tensor.transpose(thought_turn.ap[:, 0:P], t_pad[:, :], identity[:, :]))
            dve.wait(t, t_rows_free)
            t = dve.done(nc.vector.tensor_copy(t_rows[0:B * KD, :], thought_turn.ap[0:B * KD, 0:P]))
            thought_turn.free = [t]
            t_rows_free = dma(row_dram, t_rows[0:B * KD, :], dma_sem("dma_row_scratch"), t)

        def publish_thought():
            load(thought_row, thought_row.ap[:, :, :].rearrange("p b d -> p (b d)"),
                 row_dram.rearrange("k p -> (k p)").partition_broadcast(P), t_rows_free)

        def moments(source, dest, eps):
            for h in range(HALVES):
                dve.done(nc.vector.bn_stats(bn_parts[:, h, :], source[:, h * BANK:(h + 1) * BANK]))
            dve.done(nc.vector.bn_aggr(bn_out[:, 0:2], bn_parts[:, :, :]))
            t = dve.done(nc.vector.tensor_scalar(bn_out[:, 2:3], bn_out[:, 1:2], eps, None, ALU.add))
            pool.wait(t)
            t = pool.done(nc.gpsimd.tensor_tensor(dest[:, 0:1], bn_out[:, 2:3], minus_half[:, 0:1], ALU.pow))
            dve.wait(t)
            return dve.done(nc.vector.scalar_tensor_tensor(out=dest[:, 1:2], in0=bn_out[:, 0:1], scalar=-1.0,
                                                           in1=dest[:, 0:1], op0=ALU.mult, op1=ALU.mult))

        def turn_tile(source, dest):
            act.wait(dest.free)
            per = BANK // P
            for h in range(HALVES):
                bank = turn_ring.take()
                pe.wait(source.ready, bank.free)
                for s in range(per):
                    k = h * per + s
                    mm = nc.tensor.transpose(bank.ap[:, s * P:(s + 1) * P],
                                             source.ap[:, k * P:(k + 1) * P], identity[:, :])
                t = pe.done(mm)
                act.wait(t)
                t2 = act.done(nc.scalar.activation(
                    dest.ap[:, h * per:(h + 1) * per, :].rearrange("p k t -> p (k t)"),
                    bank.ap, ACT.Copy, scale=TOKEN_SCALE))
                bank.free = [t2]
            source.free.append(t)
            dest.ready, dest.free = [t2], []

        def split_tile(source, high, low, pair_free):
            dve.wait(source.ready, pair_free)
            dve.done(nc.vector.tensor_copy(high, source.ap[:, :, :]))
            t = dve.done(nc.vector.tensor_tensor(low, source.ap[:, :, :], high, ALU.subtract))
            source.free.append(t)
            return t

        def pair_product(bank, left, right):
            n = 0
            for k in range(KD):
                for a, b in ((0, 0), (0, 1), (1, 0)):
                    mm = nc.tensor.matmul(bank, left[a](k), right[b](k), start=(n == 0), stop=(n == 3 * KD - 1))
                    n += 1
                    if n == 3 * KD:
                        yield pe.done(mm)
                    elif n % KD == 0:
                        yield

        def split_weights(source_dram, waits, wide, matrix, stage):
            high, low = halves_of(wide)
            for k in range(KD):
                buf = stage.take()
                load(buf, buf.ap[:, :], source_dram[k * P:(k + 1) * P, :], *waits)
                dve.wait(buf.ready)
                t = dve.done(nc.vector.tensor_reduce(scale_stat[:, k:k + 1], buf.ap[:, :], AX_X, ALU.max,
                                                     apply_absolute_value=True))
                buf.free = [t]
                yield
            top = scale_stat[:, KD:KD + 1]
            exponent, scale = scale_stat[:, KD + 1:KD + 2], scale_stat[:, KD + 2:KD + 3]
            t = dve.done(nc.vector.tensor_reduce(top, scale_stat[:, 0:KD], AX_X, ALU.max))
            pool.wait(t)
            t = pool.done(nc.gpsimd.partition_all_reduce(exponent, top, P, bass.bass_isa.ReduceOp.max))
            dve.wait(t)
            dve.done(nc.vector.tensor_scalar(top, exponent, TINY, None, ALU.max))
            dve.done(nc.vector.tensor_scalar(exponent.bitcast(I32), top.bitcast(I32), EXPONENT_BITS, None,
                                             ALU.bitwise_and))
            dve.done(nc.vector.tensor_scalar(scale.bitcast(I32), top.bitcast(I32), EXPONENT_BITS, EXPONENT_BITS,
                                             ALU.bitwise_and, ALU.bitwise_xor))
            dve.done(nc.vector.tensor_scalar(scale, scale, WEIGHT_TOP, None, ALU.mult))
            dve.done(nc.vector.tensor_scalar(inverse[matrix][:, :], exponent,
                                             1.0 / (2.0 * WEIGHT_TOP * TOKEN_SCALE), None, ALU.mult))
            dve.wait(wide.free)
            for k in range(KD):
                buf = stage.take()
                load(buf, buf.ap[:, :], source_dram[k * P:(k + 1) * P, :])
                dve.wait(buf.ready)
                dve.done(nc.vector.tensor_scalar(high[:, k, :], buf.ap[:, :], scale, None, ALU.mult))
                t = dve.done(nc.vector.scalar_tensor_tensor(out=low[:, k, :], in0=buf.ap[:, :], scalar=scale,
                                                            in1=high[:, k, :], op0=ALU.mult, op1=ALU.subtract))
                buf.free = [t]
                yield
            wide.ready, wide.free = [t], []

        def halves_of(wide):
            v = wide.ap[:, :, :].rearrange("p k d -> p (k d)").bitcast(F16).rearrange(
                "p (h k d) -> p h k d", h=2, k=KD)
            return v[:, 0], v[:, 1]

        def side_by_side(main, other, pace):
            due = 0.0
            for _ in main:
                due += pace
                while due >= 1.0:
                    due -= 1.0
                    if other is not None and next(other, "end") == "end":
                        other = None
            for _ in other or ():
                pass

        for _ in range(len(weight_ring.buffers)):
            fetch_block()

        phase = ExitStack()
        with phase:
            gate_bias = sbuf(phase, "gate_bias", [P, D])
            gate_pair = Buffer(sbuf(phase, "gate_pair", [P, KD, D]))
            stage = ring(phase, "stage", 2, [P, D])
            x_ring = ring(phase, "x_tile", 3, [P, D])
            turned_ring = ring(phase, "turned", 2, [P, KD, P])
            pair_ring = ring(phase, "token_pair", 2, [P, 2, KD, P], F16)
            result_ring = ring(phase, "result", 2, [P, D])
            gate_bias_ready = dma(gate_bias[:, :], gate_b.partition_broadcast(P), dma_sem("dma_gate_bias"))
            wq, wk, wv = (w_attn[i * D:(i + 1) * D, :] for i in range(3))

            def fold(left, right, dest_dram):
                stored = []
                for d in range(KD):
                    res = result_ring.take()
                    for h in range(HALVES):
                        bank = product_ring.take()
                        pe.wait(left.ready, right.ready, bank.free)
                        for e in range(KD):
                            mm = nc.tensor.matmul(bank.ap, left.ap[:, e, d * P:(d + 1) * P],
                                                  right.ap[:, e, h * BANK:(h + 1) * BANK],
                                                  start=(e == 0), stop=(e == KD - 1))
                            if e % 2 and e < KD - 1:
                                yield
                        t = pe.done(mm)
                        act.wait(t, res.free)
                        t2 = act.done(nc.scalar.copy(res.ap[:, h * BANK:(h + 1) * BANK], bank.ap))
                        bank.free = [t2]
                        yield
                    res.ready, res.free = [t2], []
                    stored.append(store(res, dest_dram[d * P:(d + 1) * P, :], res.ap[:, :]))
                left.free, right.free = [t], [t]
                return stored

            def gate_tiles(tiles, matrix_pair):
                high_w, low_w = halves_of(matrix_pair)

                def fetch(tile):
                    buf = x_ring.take()
                    load(buf, buf.ap[:, :], x_flat[row_of(tile), :])
                    return buf

                def prepare(tile, buf):
                    dve.wait(buf.ready)
                    t = moments(buf.ap, token_stats[:, tile, :], EPS_OUTER)
                    act.wait(t)
                    t = act.done(nc.scalar.activation(buf.ap[:, :], buf.ap[:, :], ACT.Identity,
                                                      bias=token_stats[:, tile, 1:2],
                                                      scale=token_stats[:, tile, 0:1]))
                    buf.ready = [t]

                def turn(buf):
                    turned = turned_ring.take()
                    turn_tile(buf, turned)
                    pair = pair_ring.take()
                    pair.ready = [split_tile(turned, pair.ap[:, 0], pair.ap[:, 1], pair.free)]
                    pair.free = []
                    return pair

                bufs = {0: fetch(tiles[0]), 1: fetch(tiles[1])}
                prepare(tiles[0], bufs[0])
                pair = turn(bufs[0])
                prepare(tiles[1], bufs[1])
                for n, tile in enumerate(tiles):
                    if n + 2 < len(tiles):
                        bufs[n + 2] = fetch(tiles[n + 2])
                    following = turn(bufs[n + 1]) if n + 1 < len(tiles) else None
                    if n + 2 < len(tiles):
                        prepare(tiles[n + 2], bufs[n + 2])
                    res = result_ring.take()
                    for h in range(HALVES):
                        bank = product_ring.take()
                        cols = slice(h * BANK, (h + 1) * BANK)
                        pe.wait(pair.ready, matrix_pair.ready, bank.free)
                        for t in pair_product(bank.ap,
                                               (lambda k: pair.ap[:, 0, k, :], lambda k: pair.ap[:, 1, k, :]),
                                               (lambda k: high_w[:, k, cols], lambda k: low_w[:, k, cols])):
                            yield
                        dve.wait(t, res.free, gate_bias_ready)
                        t2 = dve.done(nc.vector.scalar_tensor_tensor(
                            out=res.ap[:, cols], in0=bank.ap, scalar=inverse["gate"][:, :],
                            in1=gate_bias[:, cols], op0=ALU.mult, op1=ALU.add))
                        bank.free = [t2]
                    pair.free = [t]
                    act.wait(t2)
                    t = act.done(nc.scalar.activation(res.ap[:, :], res.ap[:, :], ACT.Sigmoid))
                    res.ready, res.free = [t], []
                    store(res, gate1_dram[row_of(tile), :], res.ap[:, :])
                    pair = following

            def by_tiles(w):
                return w.rearrange("(e p) d -> p e d", p=P)

            def phase_1():
                load(wide_a, wide_a.ap[:, :, :], by_tiles(wk))
                load(wide_b, wide_b.ap[:, :, :], by_tiles(wq))
                yield from split_weights(gate_w, (), gate_pair, "gate", stage)
                qk_stored = yield from fold(wide_b, wide_a, qk_dram)
                load(wide_b, wide_b.ap[:, :, :], by_tiles(wv))
                act.wait(wide_a.free)
                for n in range(KD):
                    buf = stage.take()
                    load(buf, buf.ap[:, :], w_o[n * P:(n + 1) * P, :])
                    per = BANK // P
                    for h in range(HALVES):
                        bank = turn_ring.take()
                        pe.wait(buf.ready, bank.free)
                        for s in range(per):
                            e = h * per + s
                            mm = nc.tensor.transpose(bank.ap[:, s * P:(s + 1) * P],
                                                     buf.ap[:, e * P:(e + 1) * P], identity[:, :])
                        t = pe.done(mm)
                        act.wait(t)
                        t2 = act.done(nc.scalar.copy(wide_a.ap[:, h * per:(h + 1) * per, n * P:(n + 1) * P],
                                                     bank.ap.rearrange("p (k t) -> p k t", t=P)))
                        bank.free = [t2]
                    buf.free = [t]
                    yield
                wide_a.ready, wide_a.free = [t2], []
                vo_stored = yield from fold(wide_b, wide_a, vo_dram)
                yield from split_weights(qk_dram, qk_stored, wide_a, "qk", stage)
                yield from split_weights(vo_dram, vo_stored, wide_b, "vo", stage)
                yield from gate_tiles(list(range(B * NT)), gate_pair)

            side_by_side(phase_1(), think(lambda b: x[b, T - 1, :].rearrange("(k p) -> k p", p=P), None), 0.6)
            publish_thought()
            join()

        phase = ExitStack()
        with phase:
            x_ring = ring(phase, "x_in", 2, [P, D])
            g_ring = ring(phase, "g_in", 2, [P, D])
            h_ring = ring(phase, "h_tile", 2, [P, D])
            x2_ring = ring(phase, "x2_tile", 1, [P, D])
            keys_shelf = Shelf(buffers(phase, "keys", 6, [P, KD, P]))
            query_shelf = Shelf(buffers(phase, "queries", 4, [P, KD, P]))
            value_shelf = Shelf(buffers(phase, "values", 4, [P, D]))
            token_pair = Buffer(sbuf(phase, "group_pair", [P, 2, KD, GROUP * P], F16))
            stats1 = sbuf(phase, "stats1", [P, 2])
            weight_of_key = ring(phase, "weight_of_key", 2, [P, 2, P])
            high_qk, low_qk = halves_of(wide_a)
            high_vo, low_vo = halves_of(wide_b)
            groups = [(b, g) for g in reversed(range(NT // GROUP)) for b in range(B)]
            x1_stored, x2_stored, state = {}, {}, {}

            def finish_ffn(xb, gb, hb, batch, dest_stats):
                pool.wait(gb.ready, thought_row.ready)
                t = pool.done(nc.gpsimd.tensor_tensor(gb.ap[:, :], gb.ap[:, :], thought_row.ap[:, batch, :], ALU.mult))
                dve.wait(t, hb.ready)
                dve.done(nc.vector.tensor_tensor(hb.ap[:, :], hb.ap[:, :], gb.ap[:, :], ALU.add))
                gb.free = [dve.last()]
                pool.wait(hb.ready)
                t = pool.done(nc.gpsimd.tensor_tensor(xb.ap[:, :], xb.ap[:, :], half_beta[:, :], ALU.add))
                moments(hb.ap, dest_stats, EPS_FFN)
                dve.done(nc.vector.scalar_tensor_tensor(out=hb.ap[:, :], in0=hb.ap[:, :], scalar=bn_out[:, 0:1],
                                                        in1=half_gamma[:, :], op0=ALU.subtract, op1=ALU.mult))
                dve.wait(t)
                return dve.done(nc.vector.scalar_tensor_tensor(
                    out=xb.ap[:, :], in0=hb.ap[:, :], scalar=dest_stats[:, 0:1], in1=xb.ap[:, :],
                    op0=ALU.mult, op1=ALU.add))

            def make_h(tile, batch):
                xb, gb, hb = x_ring.take(), g_ring.take(), h_ring.take()
                load(xb, xb.ap[:, :], x_flat[row_of(tile), :])
                load(gb, gb.ap[:, :], gate1_dram[row_of(tile), :])
                yield
                act.wait(xb.ready, hb.free)
                hb.ready = [act.done(nc.scalar.activation(hb.ap[:, :], xb.ap[:, :], ACT.Identity,
                                                          bias=token_stats[:, tile, 1:2],
                                                          scale=token_stats[:, tile, 0:1]))]
                hb.free = []
                t = finish_ffn(xb, gb, hb, batch, stats1)
                xb.ready = [t]
                x1_stored[tile] = store(xb, x1_dram[row_of(tile), :], xb.ap[:, :])
                t = moments(xb.ap, stats1, EPS_OUTER)
                act.wait(t)
                t = act.done(nc.scalar.activation(hb.ap[:, :], xb.ap[:, :], ACT.Identity,
                                                  bias=stats1[:, 1:2], scale=stats1[:, 0:1]))
                dve.wait(t)
                hb.ready = [t]
                xb.free.append(t)
                yield hb

            def tiles_of(n):
                b, g = groups[n]
                return [b * NT + g * GROUP + i for i in range(GROUP)]

            def prepare_group(n):
                made = []
                for tile in tiles_of(n):
                    for h in make_h(tile, groups[n][0]):
                        yield
                    made.append(h)
                state["h", n] = made

            def turn_group(n):
                keys = []
                for i, h in enumerate(state.pop(("h", n))):
                    k = keys_shelf.take()
                    turn_tile(h, k)
                    free = token_pair.free if i == 0 else []
                    at = slice(i * P, (i + 1) * P)
                    t = split_tile(k, token_pair.ap[:, 0, :, at], token_pair.ap[:, 1, :, at], free)
                    keys.append(k)
                    yield
                token_pair.ready = [t]
                state["keys", n] = keys

            def queries_and_values(n):
                q = [query_shelf.take() for _ in range(GROUP)]
                v = [value_shelf.take() for _ in range(GROUP)]
                per_bank = BANK // (GROUP * P)
                for e0 in range(0, KD, per_bank):
                    bank = product_ring.take()
                    pe.wait(token_pair.ready, wide_a.ready, bank.free)
                    for e in range(e0, e0 + per_bank):
                        cols = slice(e * P, (e + 1) * P)
                        part = bank.ap[:, (e - e0) * GROUP * P:(e - e0 + 1) * GROUP * P]
                        for t in pair_product(
                                part, (lambda k: high_qk[:, k, cols], lambda k: low_qk[:, k, cols]),
                                (lambda k: token_pair.ap[:, 0, k, :], lambda k: token_pair.ap[:, 1, k, :])):
                            pass
                        yield
                    act.wait(t)
                    for i in range(GROUP):
                        if e0 == 0:
                            act.wait(q[i].free)
                        src = bank.ap.rearrange("p (e g t) -> p e g t", e=per_bank, g=GROUP)[:, :, i, :]
                        t2 = act.done(nc.scalar.activation(q[i].ap[:, e0:e0 + per_bank, :], src, ACT.Copy,
                                                           scale=query_scale[:, :]))
                    bank.free = [t2]
                for i in range(GROUP):
                    q[i].ready, q[i].free = [t2], []
                for i in range(GROUP):
                    at = slice(i * P, (i + 1) * P)
                    for h in range(HALVES):
                        bank = product_ring.take()
                        cols = slice(h * BANK, (h + 1) * BANK)
                        pe.wait(wide_b.ready, bank.free)
                        for t in pair_product(bank.ap,
                                               (lambda k: token_pair.ap[:, 0, k, at], lambda k: token_pair.ap[:, 1, k, at]),
                                               (lambda k: high_vo[:, k, cols], lambda k: low_vo[:, k, cols])):
                            yield
                        act.wait(t, v[i].free)
                        t2 = act.done(nc.scalar.activation(v[i].ap[:, cols], bank.ap, ACT.Copy,
                                                           scale=inverse["vo"][:, :]))
                        bank.free = [t2]
                    v[i].ready, v[i].free = [t2], []
                token_pair.free = [t]
                state["qv", n] = (q, v)

            def attend(tile, q, own, before):
                x2 = x2_ring.take()
                load(x2, x2.ap[:, :], x1_dram[row_of(tile), :], x1_stored[tile])
                sources = [(own, keep_own)] + ([(before, keep_prev)] if before else [])
                bank = product_ring.take()
                pe.wait(q.ready, bank.free)
                for s, ((keys, _), _) in enumerate(sources):
                    pe.wait(keys.ready)
                    for e in range(KD):
                        mm = nc.tensor.matmul(bank.ap[:, s * P:(s + 1) * P], keys.ap[:, e, :], q.ap[:, e, :],
                                              start=(e == 0), stop=(e == KD - 1))
                    t = pe.done(mm)
                    yield
                q.free.append(t)
                for (keys, _), _ in sources:
                    keys.free.append(t)
                w = weight_of_key.take()
                dve.wait(t, w.free)
                for s, (_, keep) in enumerate(sources):
                    t = dve.done(nc.vector.scalar_tensor_tensor(
                        out=w.ap[:, s, :], in0=bank.ap[:, s * P:(s + 1) * P], scalar=1.0 / TOKEN_SCALE,
                        in1=keep[:, :], op0=ALU.mult, op1=ALU.min))
                bank.free = [t]
                n = len(sources)
                t = dve.done(nc.vector.scalar_tensor_tensor(
                    out=w.ap[:, 0:n, :], in0=w.ap[:, 0:n, :], scalar=0.0, in1=w.ap[:, 0:n, :],
                    op0=ALU.max, op1=ALU.mult))
                state["w", tile] = (w, t, x2, sources)

            def collect(tile):
                w, weights_ready, x2, sources = state.pop(("w", tile))
                for h in range(HALVES):
                    cols = slice(h * BANK, (h + 1) * BANK)
                    bank = product_ring.take()
                    pe.wait(weights_ready, bank.free)
                    for s, ((_, values), _) in enumerate(sources):
                        pe.wait(values.ready)
                        mm = nc.tensor.matmul(bank.ap, w.ap[:, s, :], values.ap[:, cols],
                                              start=(s == 0), stop=(s == len(sources) - 1))
                    t = pe.done(mm)
                    dve.wait(t, x2.ready)
                    t2 = dve.done(nc.vector.tensor_tensor(x2.ap[:, cols], bank.ap, x2.ap[:, cols], ALU.add))
                    bank.free = [t2]
                    yield
                w.free = [t]
                for (_, values), _ in sources:
                    values.free.append(t)
                x2.ready = [t2]
                x2_stored[tile] = store(x2, x2_dram[row_of(tile), :], x2.ap[:, :])

            query_scale = sbuf(phase, "query_scale", [P, 1])
            act.wait(dve.done(nc.vector.tensor_scalar(query_scale[:, :], inverse["qk"][:, :], 1.0 / P, None, ALU.mult)))

            def phase_2(first, last):
                waiting = state.setdefault("waiting", {})
                if first == 0:
                    yield from prepare_group(0)
                    yield from turn_group(0)
                for n in range(first, last):
                    b, g = groups[n]
                    yield from queries_and_values(n)
                    if n + 1 < len(groups):
                        yield from prepare_group(n + 1)
                        yield from turn_group(n + 1)
                    keys, (q, v) = state.pop(("keys", n)), state.pop(("qv", n))
                    t0, t1 = tiles_of(n)
                    jobs = [(t1, q[1], (keys[1], v[1]), (keys[0], v[0]))]
                    if b in waiting:
                        wt, wq_, wown = waiting.pop(b)
                        jobs.append((wt, wq_, wown, (keys[1], v[1])))
                    if g == 0:
                        jobs.append((t0, q[0], (keys[0], v[0]), None))
                    else:
                        waiting[b] = (t0, q[0], (keys[0], v[0]))
                    for job in jobs:
                        yield from attend(*job)
                        yield from collect(job[0])
                        query_shelf.give(job[1])
                    done_with = [(keys[1], v[1])] + [j[2] for j in jobs[1:]]
                    keys_shelf.give(*(k for k, _ in done_with))
                    value_shelf.give(*(v for _, v in done_with))

            for _ in phase_2(0, B):
                pass
            last_tiles = [b * NT + NT - 1 for b in range(B)]
            side_by_side(phase_2(B, len(groups)),
                         think(lambda b: x2_dram[(b + 1) * T - 1, :].rearrange("(k p) -> k p", p=P),
                               [x2_stored[t] for t in last_tiles]), 0.45)
            join()
            publish_thought()

        phase = ExitStack()
        with phase:
            gate_bias = sbuf(phase, "gate_bias3", [P, D])
            stage = ring(phase, "stage3", 2, [P, D])
            x_ring = ring(phase, "x2_in", 4, [P, D])
            h_ring = ring(phase, "h2_tile", 4, [P, D])
            turned_ring = ring(phase, "turned3", 2, [P, KD, P])
            pair_ring = ring(phase, "token_pair3", 2, [P, 2, KD, P], F16)
            g_ring = ring(phase, "gate3", 2, [P, D])
            stats1 = sbuf(phase, "stats3", [P, 2])
            gate_bias_ready = dma(gate_bias[:, :], gate_b.partition_broadcast(P), dma_sem("dma_gate_bias"))
            high_w, low_w = halves_of(wide_a)
            wide_a.free = []
            for _ in split_weights(gate_w, (), wide_a, "gate", stage):
                pass

            def fetch3(tile):
                xb = x_ring.take()
                load(xb, xb.ap[:, :], x2_dram[row_of(tile), :])
                return xb

            def prepare3(tile, xb):
                hb = h_ring.take()
                dve.wait(xb.ready)
                t = moments(xb.ap, token_stats[:, tile, :], EPS_OUTER)
                act.wait(t, hb.free)
                t = act.done(nc.scalar.activation(hb.ap[:, :], xb.ap[:, :], ACT.Identity,
                                                  bias=token_stats[:, tile, 1:2], scale=token_stats[:, tile, 0:1]))
                hb.ready, hb.free = [t], []
                return xb, hb

            def turn3(hb):
                turned, pair = turned_ring.take(), pair_ring.take()
                turn_tile(hb, turned)
                pair.ready = [split_tile(turned, pair.ap[:, 0], pair.ap[:, 1], pair.free)]
                pair.free = []
                return pair

            def end3(tile, xb, hb, gb):
                dve.wait(hb.free)
                t = finish_ffn(xb, gb, hb, tile // NT, stats1)
                hb.free, xb.ready = [t], [t]
                store(xb, out_flat[row_of(tile), :], xb.ap[:, :])

            tiles = list(range(B * NT))
            loaded = {n: fetch3(tiles[n]) for n in range(3)}
            ready = {n: prepare3(tiles[n], loaded[n]) for n in range(2)}
            pairs = {0: turn3(ready[0][1])}
            previous = None
            for n, tile in enumerate(tiles):
                if n + 1 < len(tiles):
                    pairs[n + 1] = turn3(ready[n + 1][1])
                pair, gb = pairs.pop(n), g_ring.take()
                for h in range(HALVES):
                    bank = product_ring.take()
                    cols = slice(h * BANK, (h + 1) * BANK)
                    pe.wait(pair.ready, wide_a.ready, bank.free)
                    for t in pair_product(bank.ap,
                                           (lambda k: pair.ap[:, 0, k, :], lambda k: pair.ap[:, 1, k, :]),
                                           (lambda k: high_w[:, k, cols], lambda k: low_w[:, k, cols])):
                        pass
                    dve.wait(t, gb.free, gate_bias_ready)
                    t2 = dve.done(nc.vector.scalar_tensor_tensor(
                        out=gb.ap[:, cols], in0=bank.ap, scalar=inverse["gate"][:, :],
                        in1=gate_bias[:, cols], op0=ALU.mult, op1=ALU.add))
                    bank.free = [t2]
                pair.free = [t]
                act.wait(t2)
                gb.ready = [act.done(nc.scalar.activation(gb.ap[:, :], gb.ap[:, :], ACT.Sigmoid))]
                gb.free = []
                if n + 2 < len(tiles):
                    ready[n + 2] = prepare3(tiles[n + 2], loaded.pop(n + 2))
                xb, hb = ready.pop(n)
                end3(tile, xb, hb, gb)
                if n + 3 < len(tiles):
                    loaded[n + 3] = fetch3(tiles[n + 3])
            join()


_INS = ['x', 'w_attn', 'w_o', 'in_gamma', 'in_beta', 'agg_w', 'agg_b', 'pn_gamma', 'pn_beta', 'd1_w', 'd1_b',
        'd2_w', 'd2_b', 'bc_w', 'bc_b', 'gate_w', 'gate_b', 'out_gamma', 'out_beta']


def kernel(**inputs):
    import numpy as _np
    import concourse.bacc as _bacc
    from concourse import mybir as _mybir
    from concourse.bass_utils import run_bass_kernel_spmd as _run

    nc = _bacc.Bacc("TRN2", target_bir_lowering=False, num_devices=1)
    arrays, args = {}, []
    for name in _INS:
        full = ("L0_attn_" if name in ("x", "w_attn", "w_o") else "L0_ffn_") + name
        a = _np.ascontiguousarray(inputs[full])
        arrays[f"in_{name}"] = a
        args.append(nc.dram_tensor(f"in_{name}", a.shape, _mybir.dt.from_np(a.dtype), kind="ExternalInput").ap())
    shape = inputs["L0_attn_x"].shape
    args.append(nc.dram_tensor("out_0", shape, _mybir.dt.float32, kind="ExternalOutput").ap())
    macaron_kernel(nc, *args)
    r = _run(nc, [arrays], core_ids=[0])
    return r.results[0]["out_0"]
```

```python
from contextlib import ExitStack
from itertools import accumulate

import concourse.bass as bass
from concourse import mybir

F32 = mybir.dt.float32
F16 = mybir.dt.float16
BF16 = mybir.dt.bfloat16
I32 = mybir.dt.int32
ALU = mybir.AluOpType
ACT = mybir.ActivationFunctionType
AX_X = mybir.AxisListType.X

P = 128
BANK = 512
PE_COLS = 32
K_STEPS = 4
TILE_DONE = "tile done"
SLACK = 2
STORE_DELAY = 6
RATIO_A = 0.6
WAIT_GATE = 3
WAIT_X = 2
PACE_1 = 0.6
PACE_2 = 0.65
EPS_OUTER = 1e-5
EPS_FFN = 1e-6
TOKEN_SCALE = 1024.0
EXPONENT_BITS = 0x7F800000
WEIGHT_TOP = 8192.0
TINY = 2.0 ** -100
NEVER = 3.0e38


class Ticket:

    def __init__(self, sem, value):
        self.sem, self.value = sem, value


class Stream:

    def __init__(self, eng, sem, serial):
        self.eng, self.sem, self.count, self.serial, self.seen = eng, sem, 0, serial, {}

    def wait(self, *tickets):
        for t in tickets:
            if isinstance(t, (list, tuple)):
                self.wait(*t)
            elif t is not None and self.seen.get(t.sem.name, 0) < t.value:
                self.eng.wait_ge(t.sem, t.value)
                self.seen[t.sem.name] = t.value

    def done(self, instruction):
        instruction.then_inc(self.sem, 1)
        self.count += 1
        t = Ticket(self.sem, self.count)
        if self.serial:
            self.wait(t)
        return t

    def last(self):
        return Ticket(self.sem, self.count) if self.count else None


class Buffer:

    def __init__(self, ap, dma_sem=None):
        self.ap, self.dma_sem, self.dma_count = ap, dma_sem, 0
        self.ready, self.free = [], []


class Ring:
    def __init__(self, buffers):
        self.buffers, self.at = buffers, 0

    def take(self):
        self.at += 1
        return self.buffers[(self.at - 1) % len(self.buffers)]


class Shelf:

    def __init__(self, buffers):
        self.free = list(buffers)

    def take(self):
        return self.free.pop(0)

    def give(self, *buffers):
        self.free.extend(buffers)


def macaron_kernel(nc, x, w_attn, w_o, in_gamma, in_beta, agg_w, agg_b, pn_gamma, pn_beta,
                   d1_w, d1_b, d2_w, d2_b, bc_w, bc_b, gate_w, gate_b, out_gamma, out_beta, out):
    B, T, D = x.shape
    H = d1_w.shape[1]
    KD, KH = D // P, H // P
    NT = T // P
    HALVES = D // BANK
    GROUP = 2
    WCHUNK = 2 * D
    assert B == 2 and D == 1024 and H % WCHUNK == 0 and NT % GROUP == 0

    x_flat, out_flat = (a.rearrange("b t d -> (b t) d") for a in (x, out))
    row_of = lambda tile: slice(tile * P, (tile + 1) * P)
    gate1_dram = nc.dram_tensor("gate1_scratch", [B * T, D], F32, kind="Internal").ap()
    x1_dram = nc.dram_tensor("x1_scratch", [B * T, D], F32, kind="Internal").ap()
    x2_dram = nc.dram_tensor("x2_scratch", [B * T, D], F32, kind="Internal").ap()
    qk_dram = nc.dram_tensor("qk_scratch", [D, D], F32, kind="Internal").ap()
    vo_dram = nc.dram_tensor("vo_scratch", [D, D], F32, kind="Internal").ap()
    gate_pair_dram = nc.dram_tensor("gate_pair_scratch", [P, KD * D], F32, kind="Internal").ap()
    row_dram = nc.dram_tensor("row_scratch", [B * KD, P], F32, kind="Internal").ap()

    whole = ExitStack()
    with whole:
        every_dma = []

        def new_sem(name):
            return whole.enter_context(nc.semaphore(name))

        pe = Stream(nc.tensor, new_sem("pe_done"), serial=False)
        act = Stream(nc.scalar, new_sem("act_done"), serial=True)
        dve = Stream(nc.vector, new_sem("dve_done"), serial=True)
        pool = Stream(nc.gpsimd, new_sem("pool_done"), serial=True)
        sp = Stream(nc.sync, new_sem("sp_done"), serial=False)
        engines = (pe, act, dve, pool, sp)

        def sbuf(stack, name, shape, dtype=F32):
            return stack.enter_context(nc.sbuf_tensor(name, shape, dtype))

        dma_sems = {}

        def dma_sem(name):
            if name not in dma_sems:
                dma_sems[name] = [new_sem(name), 0]
            return dma_sems[name]

        late_stores = []
        steps_made = [0]

        def issue_stores(up_to):
            while late_stores and up_to(late_stores[0]):
                late_stores.pop(0)[1]()

        def tick():
            steps_made[0] += 1
            issue_stores(lambda s: s[2] <= steps_made[0])

        def flat(tickets):
            for t in tickets:
                if isinstance(t, (list, tuple)):
                    yield from flat(t)
                elif t is not None:
                    yield t

        def dma(to, source, sem, *waits):
            for t in flat(waits):
                while any(t is s[0] for s in late_stores):
                    late_stores.pop(0)[1]()
            sp.wait(*waits)
            nc.sync.dma_start(to, source).then_inc(sem[0], 16)
            sem[1] += 16
            return Ticket(sem[0], sem[1])

        def buffers(stack, name, n, shape, dtype=F32):
            return [Buffer(sbuf(stack, f"{name}{i}", shape, dtype), dma_sem(f"dma_{name}{i}"))
                    for i in range(n)]

        def as_features(buf):
            return buf.ap.rearrange("p (k t) -> p k t", t=P)

        def as_pair(ap):
            return ap.bitcast(F16).rearrange("p (h k t) -> p h k t", h=2, k=KD)

        def load(buf, to, source, *waits):
            buf.ready = [dma(to, source, buf.dma_sem, buf.free, *waits)]
            buf.free = []

        def store(buf, to, source):
            sem, ready = buf.dma_sem, buf.ready
            sem[1] += 16
            t = Ticket(sem[0], sem[1])

            def issue():
                sp.wait(ready)
                nc.sync.dma_start(to, source).then_inc(sem[0], 16)

            late_stores.append((t, issue, steps_made[0] + STORE_DELAY))
            buf.free.append(t)
            return t

        product_banks = whole.enter_context(nc.psum_tensor("product_banks", [P, 4, BANK], F32))
        turn_banks = whole.enter_context(nc.psum_tensor("turn_banks", [P, 2, BANK], F32))
        thought_acc = Buffer(whole.enter_context(nc.psum_tensor("thought_acc", [P, BANK], F32))[:, :])
        thought_turn = Buffer(whole.enter_context(nc.psum_tensor("thought_turn", [P, BANK], F32))[:, :])
        product_ring = Ring([Buffer(product_banks[:, i, :]) for i in range(4)])
        turn_ring = Ring([Buffer(turn_banks[:, i, :]) for i in range(2)])

        identity = sbuf(whole, "identity", [P, P])
        mean_maker = sbuf(whole, "mean_maker", [P, P])
        keep_prev = sbuf(whole, "keep_prev", [P, P], BF16)
        keep_own = sbuf(whole, "keep_own", [P, P], BF16)
        minus_half = sbuf(whole, "minus_half", [P, 2])
        half_gamma = sbuf(whole, "half_gamma", [P, D])
        half_beta = sbuf(whole, "half_beta", [P, D])
        thought_row = Buffer(sbuf(whole, "thought_row", [P, B, D]), dma_sem("dma_thought_row"))
        token_stats = sbuf(whole, "token_stats", [P, B * NT, 2])
        bn_parts = sbuf(whole, "bn_parts", [P, HALVES, 6])
        weight_ring = Ring(buffers(whole, "thought_weights", 3, [P, WCHUNK]))
        wide_a = Buffer(sbuf(whole, "wide_a", [P, KD, D]), dma_sem("dma_wide_a"))
        wide_b = Buffer(sbuf(whole, "wide_b", [P, KD, D]), dma_sem("dma_wide_b"))
        thought = sbuf(whole, "thought", [P, B, KD])
        centred = sbuf(whole, "centred", [P, B, KD])
        squares = sbuf(whole, "squares", [P, B, KD])
        t_small = sbuf(whole, "t_small", [P, 3, B])
        hidden = sbuf(whole, "hidden", [P, B, KH])
        spread = sbuf(whole, "spread", [P, B, KD])
        narrow_in = sbuf(whole, "narrow_in", [P, KD, B])
        narrow_hidden = sbuf(whole, "narrow_hidden", [P, KH, B])
        t_wide = Buffer(sbuf(whole, "t_wide", [P, BANK]))
        t_rows = t_wide.ap[:, 0:P]
        vectors = sbuf(whole, "vectors", [P, P])
        d1_bias = sbuf(whole, "d1_bias", [P, KH])
        scale_stat = {m: sbuf(whole, f"scale_stat_{m}", [P, KD + 3]) for m in ("gate", "qk", "vo")}
        key_weights = Ring(buffers(whole, "key_weights", 2, [P, 2, P]))
        query_scale = sbuf(whole, "query_scale", [P, 1])
        stat_ring = Ring([Buffer(sbuf(whole, f"stats{i}", [P, 8])[:, :]) for i in range(4)])
        TILES = 24
        arena = sbuf(whole, "arena", [P, TILES, D])
        gate_pair = Buffer(arena[:, 0:KD, :])
        group_pair = Buffer(arena[:, TILES - 2:TILES, :])
        shelf = Shelf([Buffer(arena[:, i, :], dma_sem(f"dma_tile{i}")) for i in range(KD, TILES - 2)])
        inverse = {m: sbuf(whole, f"inverse_{m}", [P, 1]) for m in ("gate", "qk", "vo")}

        def load_piece(buf, source, e):
            if e == 0:
                buf.piece_ready = []
            buf.piece_ready.append(dma(buf.ap[:, e, :], source[e * P:(e + 1) * P, :],
                                       dma_sem(f"{buf.name}_piece{e}"), buf.free))

        def fold(left, right, dest_dram, stored, matrix):
            sizes = [2] + [1] * (KD - 2)
            for d0, size in zip(accumulate([0] + sizes), sizes):
                banks = [product_ring.take() for _ in range(size * HALVES)]
                pe.wait(*(bank.free for bank in banks))
                for e in range(KD):
                    pe.wait(left.piece_ready[e], right.piece_ready[e])
                    for n, bank in enumerate(banks):
                        d, h = d0 + n // HALVES, n % HALVES
                        mm = nc.tensor.matmul(bank.ap, left.ap[:, e, d * P:(d + 1) * P],
                                              right.ap[:, e, h * BANK:(h + 1) * BANK],
                                              start=(e == 0), stop=(e == KD - 1))
                        if n == 1 and size > 1:
                            yield
                    t = pe.done(mm)
                    yield
                for i in range(size):
                    res = shelf.take()
                    act.wait(t, res.free)
                    for h in range(HALVES):
                        t2 = act.done(nc.scalar.copy(res.ap[:, h * BANK:(h + 1) * BANK],
                                                     banks[i * HALVES + h].ap))
                        banks[i * HALVES + h].free = [t2]
                    res.ready, res.free = [t2], []
                    d = d0 + i
                    note_largest(res, matrix, d)
                    stored.append(store(res, dest_dram[d * P:(d + 1) * P, :], res.ap))
                    shelf.give(res)
            left.free, right.free = [t], [t]

        def note_largest(buf, matrix, k):
            dve.wait(buf.ready)
            t = dve.done(nc.vector.tensor_reduce(scale_stat[matrix][:, k:k + 1], buf.ap, AX_X, ALU.max,
                                                 apply_absolute_value=True))
            buf.free.append(t)

        pool.done(nc.gpsimd.memset(identity[:, :], 0.0))
        pool.done(nc.gpsimd.affine_select(out=identity[:, :], in_=identity[:, :], compare_op=ALU.not_equal,
                                          fill=1.0, base=0, pattern=[[-1, P]], channel_multiplier=1))
        for keep in (keep_prev, keep_own):
            pool.done(nc.gpsimd.memset(keep[:, :], NEVER))
        pool.done(nc.gpsimd.affine_select(out=keep_prev[:, :], in_=keep_prev[:, :], compare_op=ALU.is_ge,
                                          fill=0.0, base=0, pattern=[[-1, P]], channel_multiplier=1))
        constants = pool.done(nc.gpsimd.affine_select(
            out=keep_own[:, :], in_=keep_own[:, :], compare_op=ALU.is_ge,
            fill=0.0, base=0, pattern=[[1, P]], channel_multiplier=-1))
        dve.done(nc.vector.memset(mean_maker[:, :], 1.0 / D))
        dve.done(nc.vector.memset(minus_half[:, :], -0.5))
        dve.done(nc.vector.memset(thought_acc.ap, 0.0))
        zeroed = dve.done(nc.vector.memset(t_wide.ap[:, :], 0.0))
        wq, wk, wv = (w_attn[i * D:(i + 1) * D, :] for i in range(3))
        FIRST_PIECES = 2
        wide_a.name, wide_b.name = "wide_a", "wide_b"
        for e in range(FIRST_PIECES):
            load_piece(wide_b, wq, e)
            load_piece(wide_a, wk, e)

        qk_stored, vo_stored, gate_stored = [], [], {}
        first_fold = fold(wide_b, wide_a, qk_dram, qk_stored, "qk")
        for _ in range(2 * FIRST_PIECES):
            next(first_fold)
        pe.wait(constants, zeroed)

        def turn_rows(rows_ready, dest, n):
            pe.wait(rows_ready, thought_turn.free)
            t = pe.done(nc.tensor.transpose(thought_turn.ap[:, 0:P], t_rows, identity[:, :]))
            t_wide.free = [t]
            dve.wait(t)
            t = dve.done(nc.vector.tensor_copy(dest, thought_turn.ap[:, 0:n]))
            thought_turn.free = [t]
            return t

        names = (in_gamma, in_beta, agg_b, pn_gamma, pn_beta, d2_b, bc_b)
        sp.wait(zeroed)
        for v, vec in enumerate(names):
            for b in range(B):
                at = (v * B + b) * KD
                rows = dma(t_rows[at:at + KD, :], vec.rearrange("(k p) -> k p", p=P),
                           dma_sem("dma_vectors"))
        turned = turn_rows(rows, vectors[:, 0:len(names) * B * KD], len(names) * B * KD)
        rows = dma(t_rows[0:KH, :], d1_b.rearrange("(k p) -> k p", p=P), dma_sem("dma_d1_bias"), turned)
        turn_rows(rows, d1_bias[:, :], KH)
        V_IN_G, V_IN_B, V_AGG_B, V_PN_G, V_PN_B, V_D2_B, V_BC_B = range(len(names))
        vector_of = lambda v, b: vectors[:, (v * B + b) * KD:(v * B + b + 1) * KD]

        def weight_blocks():
            def narrow(w, tiles):
                for k in range(0, tiles, 2):
                    yield w[k * P:(k + 2) * P, :].rearrange("(k p) n -> p k n", p=P)

            def wide(w):
                for c in range(H // WCHUNK):
                    for k in range(KD):
                        yield w[k * P:(k + 1) * P, c * WCHUNK:(c + 1) * WCHUNK]

            for _ in range(2):
                yield from narrow(agg_w, KD)
                for _ in range(K_STEPS):
                    yield from wide(d1_w)
                    yield from narrow(d2_w, KH)
                yield from narrow(bc_w, KD)

        blocks = weight_blocks()
        pending = []

        def fetch_block():
            source = next(blocks, None)
            if source is not None:
                buf = weight_ring.take()
                to = buf.ap[:, :]
                if len(source.shape) == 3:
                    to = to.rearrange("p (k n) -> p k n", k=2)
                load(buf, to, source)
                pending.append(buf)

        def next_block():
            return pending.pop(0)

        def used_block(buf, t):
            buf.free = [t]
            fetch_block()

        def slack():
            for _ in range(SLACK):
                yield

        def norm_thought(source, dest, eps, ready, gamma=None, beta=None):
            pe.wait(ready, thought_turn.free)
            t = pe.done(nc.tensor.matmul(thought_turn.ap[:, 0:B * KD], mean_maker[:, :],
                                         source[:, :, :].rearrange("p b k -> p (b k)"), start=True, stop=True))
            sums = thought_turn.ap[:, 0:B * KD].rearrange("p (b k) -> p b k", b=B)
            dve.wait(t)
            dve.done(nc.vector.tensor_reduce(t_small[:, 0, :], sums, AX_X, ALU.add))
            for b in range(B):
                dve.done(nc.vector.tensor_scalar(centred[:, b, :], source[:, b, :], t_small[:, 0, b:b + 1],
                                                 None, ALU.subtract))
            t = dve.done(nc.vector.tensor_tensor(squares[:, :, :], centred[:, :, :], centred[:, :, :], ALU.mult))
            yield from slack()
            pe.wait(t)
            t = pe.done(nc.tensor.matmul(thought_turn.ap[:, 0:B * KD], mean_maker[:, :],
                                         squares[:, :, :].rearrange("p b k -> p (b k)"), start=True, stop=True))
            dve.wait(t)
            t = dve.done(nc.vector.tensor_reduce(t_small[:, 1, :], sums, AX_X, ALU.add))
            thought_turn.free = [t]
            t = dve.done(nc.vector.tensor_scalar(t_small[:, 1, :], t_small[:, 1, :], eps, None, ALU.add))
            pool.wait(t)
            t = pool.done(nc.gpsimd.tensor_tensor(t_small[:, 2, :], t_small[:, 1, :], minus_half[:, 0:B], ALU.pow))
            dve.wait(t)
            for b in range(B):
                scaled = centred[:, b, :] if gamma is not None else dest(b)
                if gamma is None:
                    t = dve.done(nc.vector.tensor_scalar(dest(b), centred[:, b, :], t_small[:, 2, b:b + 1],
                                                         None, ALU.mult))
                else:
                    dve.done(nc.vector.scalar_tensor_tensor(
                        out=scaled, in0=centred[:, b, :], scalar=t_small[:, 2, b:b + 1],
                        in1=vector_of(gamma, b), op0=ALU.mult, op1=ALU.mult))
                    t = dve.done(nc.vector.tensor_tensor(dest(b), scaled, vector_of(beta, b), ALU.add))
            yield from slack()
            yield t

        def turn_sums(t):
            dve.wait(t, t_wide.free)
            t = dve.done(nc.vector.tensor_copy(t_wide.ap[:, :], thought_acc.ap[:, :]))
            thought_acc.free = [t]
            yield from slack()
            pe.wait(t, thought_turn.free)
            for s in range(BANK // P):
                mm = nc.tensor.transpose(thought_turn.ap[:, s * P:(s + 1) * P],
                                         t_wide.ap[:, s * P:(s + 1) * P], identity[:, :])
            t = pe.done(mm)
            t_wide.free = [t]
            yield t

        def turned_view(j, b):
            return thought_turn.ap.rearrange("p (s r) -> p s r", r=P)[:, :, PE_COLS * j + b]

        def narrow_product(stationary, tiles, ready, finish):
            pe.wait(ready, thought_acc.free)
            for i in range(0, tiles, 2):
                buf = next_block()
                pe.wait(buf.ready)
                w = buf.ap[:, :].rearrange("p (k n) -> p k n", k=2)
                for a in range(2):
                    for h in range(HALVES):
                        j = 2 * a + h
                        mm = nc.tensor.matmul(thought_acc.ap[PE_COLS * j:PE_COLS * j + B, :],
                                              stationary[:, i + a, :], w[:, a, h * BANK:(h + 1) * BANK],
                                              start=(i == 0), stop=(i == tiles - 2))
                t = pe.done(mm)
                used_block(buf, t)
                yield
            for t in turn_sums(t):
                yield
            dve.wait(t)
            per = BANK // P
            for b in range(B):
                for h in range(HALVES):
                    both = thought_turn.ap.rearrange("p (s a r) -> p s a r", a=2, r=2 * PE_COLS)[
                        :, :, :, PE_COLS * h + b]
                    t = dve.done(nc.vector.tensor_reduce(squares[:, b, h * per:(h + 1) * per], both, AX_X, ALU.add))
            thought_turn.free = [t]
            finish()
            yield from slack()

        def add_bias(bias, dest):
            def go():
                for b in range(B):
                    dve.done(nc.vector.tensor_tensor(dest[:, b, :], squares[:, b, :], vector_of(bias, b), ALU.add))
            return go

        def add_step():
            add_bias(V_D2_B, squares)()
            dve.done(nc.vector.tensor_tensor(thought[:, :, :], thought[:, :, :], squares[:, :, :], ALU.add))

        def wide_product(ready):
            for c in range(H // WCHUNK):
                pe.wait(ready, thought_acc.free)
                for k in range(KD):
                    buf = next_block()
                    pe.wait(buf.ready)
                    for j in range(WCHUNK // BANK):
                        mm = nc.tensor.matmul(thought_acc.ap[PE_COLS * j:PE_COLS * j + B, :],
                                              narrow_in[:, k, :], buf.ap[:, j * BANK:(j + 1) * BANK],
                                              start=(k == 0), stop=(k == KD - 1))
                    t = pe.done(mm)
                    used_block(buf, t)
                    yield
                for t in turn_sums(t):
                    yield
                dve.wait(t)
                per = BANK // P
                for b in range(B):
                    for j in range(WCHUNK // BANK):
                        at = (c * (WCHUNK // BANK) + j) * per
                        t = dve.done(nc.vector.tensor_tensor(hidden[:, b, at:at + per], turned_view(j, b),
                                                             d1_bias[:, at:at + per], ALU.add))
                thought_turn.free = [t]
            act.wait(t, pe.last())
            for b in range(B):
                t = act.done(nc.scalar.activation(narrow_hidden[:, :, b], hidden[:, b, :], ACT.Gelu))
            yield from slack()
            yield t

        def think(source_rows, ready):
            for b in range(B):
                rows = dma(t_rows[b * KD:(b + 1) * KD, :], source_rows(b), dma_sem("dma_thought_in"),
                           ready, t_wide.free)
            t = turn_rows(rows, thought[:, :, :].rearrange("p b k -> p (b k)"), B * KD)
            yield
            into_thought = lambda b: thought[:, b, :]
            into_narrow = lambda b: narrow_in[:, :, b]
            for t in norm_thought(thought, into_thought, EPS_OUTER, t):
                yield
            for t in norm_thought(thought, into_narrow, EPS_FFN, t, V_IN_G, V_IN_B):
                yield
            yield from narrow_product(narrow_in, KD, t, add_bias(V_AGG_B, thought))
            for _ in range(K_STEPS):
                for t in norm_thought(thought, into_narrow, EPS_FFN, dve.last(), V_PN_G, V_PN_B):
                    yield
                for t in wide_product(t):
                    yield
                yield from narrow_product(narrow_hidden, KH, t, add_step)
            for b in range(B):
                t = dve.done(nc.vector.tensor_copy(narrow_in[:, :, b], thought[:, b, :]))
            yield from narrow_product(narrow_in, KD, t, add_bias(V_BC_B, spread))
            pe.wait(dve.last(), thought_turn.free)
            t = pe.done(nc.tensor.matmul(thought_turn.ap[0:B * KD, 0:P], spread[:, :, :].rearrange("p b k -> p (b k)"),
                                         identity[:, :], start=True, stop=True))
            dve.wait(t, t_wide.free)
            t = dve.done(nc.vector.tensor_copy(t_rows[0:B * KD, :], thought_turn.ap[0:B * KD, 0:P]))
            thought_turn.free = [t]
            t_wide.free = [dma(row_dram, t_rows[0:B * KD, :], dma_sem("dma_row_scratch"), t)]

        def publish_thought():
            load(thought_row, thought_row.ap[:, :, :].rearrange("p b d -> p (b d)"),
                 row_dram.rearrange("k p -> (k p)").partition_broadcast(P), t_wide.free)

        def moments(source, eps):
            st = stat_ring.take()
            dve.wait(st.free)
            for h in range(HALVES):
                dve.done(nc.vector.bn_stats(bn_parts[:, h, :], source[:, h * BANK:(h + 1) * BANK]))
            dve.done(nc.vector.bn_aggr(st.ap[:, 0:2], bn_parts[:, :, :]))
            t = dve.done(nc.vector.tensor_scalar(st.ap[:, 2:3], st.ap[:, 1:2], eps, None, ALU.add))
            st.ready, st.free = [t], []
            return st

        def one_over_std(st, dest):
            pool.wait(st.ready)
            return pool.done(nc.gpsimd.tensor_tensor(dest, st.ap[:, 2:3], minus_half[:, 0:1], ALU.pow))

        def normalisers(source, dest, eps):
            st = moments(source, eps)
            t = dve.done(nc.vector.tensor_scalar(st.ap[:, 3:4], st.ap[:, 0:1], -1.0, None, ALU.mult))
            one_over_std(st, dest[:, 0:1])
            pool.wait(t)
            t = pool.done(nc.gpsimd.tensor_tensor(dest[:, 1:2], st.ap[:, 3:4], dest[:, 0:1], ALU.mult))
            st.free = [t]
            return t

        def turn_tile(source, dest):
            per = BANK // P
            for h in range(HALVES):
                bank = turn_ring.take()
                pe.wait(source.ready, bank.free)
                for s in range(per):
                    k = h * per + s
                    mm = nc.tensor.transpose(bank.ap[:, s * P:(s + 1) * P],
                                             source.ap[:, k * P:(k + 1) * P], identity[:, :])
                t = pe.done(mm)
                act.wait(t, dest.free)
                t2 = act.done(nc.scalar.activation(dest.ap[:, h * BANK:(h + 1) * BANK], bank.ap, ACT.Copy,
                                                   scale=TOKEN_SCALE))
                bank.free = [t2]
                if h < HALVES - 1:
                    yield
            source.free.append(t)
            dest.ready, dest.free = [t2], []
            yield

        def split_tile(source, high, low, pair_free):
            dve.wait(source.ready, pair_free)
            dve.done(nc.vector.tensor_copy(high, as_features(source)))
            t = dve.done(nc.vector.tensor_tensor(low, as_features(source), high, ALU.subtract))
            source.free.append(t)
            return t

        def pair_product(bank, left, right):
            n = 0
            for k in range(KD):
                for a, b in ((0, 0), (0, 1), (1, 0)):
                    mm = nc.tensor.matmul(bank, left[a](k), right[b](k), start=(n == 0), stop=(n == 3 * KD - 1))
                    n += 1
                    if n == 3 * KD:
                        yield pe.done(mm)
                    elif n % KD == 0:
                        yield

        def split_weights(matrix, wide, fetch_rows, ahead):
            high, low = halves_of(wide)
            rows = [fetch_rows(k) for k in range(ahead)]
            stat = scale_stat[matrix]
            top, exponent, scale = (stat[:, KD + i:KD + i + 1] for i in range(3))
            t = dve.done(nc.vector.tensor_reduce(top, stat[:, 0:KD], AX_X, ALU.max))
            pool.wait(t)
            t = pool.done(nc.gpsimd.partition_all_reduce(exponent, top, P, bass.bass_isa.ReduceOp.max))
            for _ in range(2):
                yield
            dve.wait(t)
            dve.done(nc.vector.tensor_scalar(top, exponent, TINY, None, ALU.max))
            dve.done(nc.vector.tensor_scalar(exponent.bitcast(I32), top.bitcast(I32), EXPONENT_BITS, None,
                                             ALU.bitwise_and))
            dve.done(nc.vector.tensor_scalar(scale.bitcast(I32), top.bitcast(I32), EXPONENT_BITS, EXPONENT_BITS,
                                             ALU.bitwise_and, ALU.bitwise_xor))
            dve.done(nc.vector.tensor_scalar(scale, scale, WEIGHT_TOP, None, ALU.mult))
            dve.done(nc.vector.tensor_scalar(inverse[matrix][:, :], exponent,
                                             1.0 / (2.0 * WEIGHT_TOP * TOKEN_SCALE), None, ALU.mult))
            dve.wait(wide.free)
            for k in range(KD):
                yield
                buf = rows.pop(0)
                dve.wait(buf.ready)
                dve.done(nc.vector.tensor_scalar(high[:, k, :], buf.ap, scale, None, ALU.mult))
                t = dve.done(nc.vector.scalar_tensor_tensor(out=low[:, k, :], in0=buf.ap, scalar=scale,
                                                            in1=high[:, k, :], op0=ALU.mult, op1=ALU.subtract))
                buf.free.append(t)
                shelf.give(buf)
                if k + ahead < KD:
                    rows.append(fetch_rows(k + ahead))
            wide.ready, wide.free = [t], []
            yield

        def split_gate():
            rows = [fetch_feature_tile(gate_w, k) for k in range(KD)]
            for _ in range(WAIT_GATE):
                yield
            for k in range(KD):
                yield
                note_largest(rows[k], "gate", k)
            yield from split_weights("gate", gate_pair, lambda k: rows[k], KD)

        def fetch_feature_tile(source, k, *waits):
            buf = shelf.take()
            load(buf, buf.ap, source[k * P:(k + 1) * P, :], *waits)
            return buf

        def halves_of(wide):
            v = wide.ap[:, :, :].rearrange("p k d -> p (k d)").bitcast(F16).rearrange(
                "p (h k d) -> p h k d", h=2, k=KD)
            return v[:, 0], v[:, 1]

        def alongside(main, other, pace):
            due = 0.0
            for _ in main:
                tick()
                yield
                due += pace
                while due >= 1.0:
                    due -= 1.0
                    next(other, None)
            for _ in other:
                tick()
                yield

        def run(steps):
            for _ in steps:
                tick()

        think_1 = think(lambda b: x[b, T - 1, :].rearrange("(k p) -> k p", p=P), None)
        next(think_1)


        def load_second_fold():
            per, ahead = BANK // P, 3
            rows = []

            def fetch_rows(n):
                if n < KD:
                    buf = shelf.take()
                    load(buf, buf.ap, w_o[n * P:(n + 1) * P, :])
                    rows.append(buf)

            for n in range(ahead):
                fetch_rows(n)
            yield
            for n in range(KD):
                fetch_rows(n + ahead)
                load_piece(wide_b, wv, n)
                buf = rows.pop(0)
                for h in range(HALVES):
                    bank = turn_ring.take()
                    pe.wait(buf.ready, bank.free)
                    for s in range(per):
                        e = h * per + s
                        mm = nc.tensor.transpose(bank.ap[:, s * P:(s + 1) * P],
                                                 buf.ap[:, e * P:(e + 1) * P], identity[:, :])
                    t = pe.done(mm)
                    act.wait(t, wide_a.free)
                    t2 = act.done(nc.scalar.copy(wide_a.ap[:, h * per:(h + 1) * per, n * P:(n + 1) * P],
                                                 bank.ap.rearrange("p (k t) -> p k t", t=P)))
                    bank.free = [t2]
                    yield
                buf.free = [t]
                shelf.give(buf)
            wide_a.piece_ready = [t2] * KD

        def fetch(tile, source, *waits):
            buf = shelf.take()
            load(buf, buf.ap, source[row_of(tile), :], *waits)
            return buf

        def normalise(source, dest, stats, eps):
            dve.wait(source.ready)
            t = normalisers(source.ap, stats, eps)
            act.wait(t, source.ready, dest.free)
            t = act.done(nc.scalar.activation(dest.ap, source.ap, ACT.Identity,
                                              bias=stats[:, 1:2], scale=stats[:, 0:1]))
            dest.ready, dest.free = [t], []
            return t

        def turn_and_split(h):
            pair = shelf.take()
            halves = as_pair(pair.ap)
            per = BANK // P
            act.wait(pair.free)
            for half in range(HALVES):
                bank = turn_ring.take()
                pe.wait(h.ready, bank.free)
                for s in range(per):
                    k = half * per + s
                    mm = nc.tensor.transpose(bank.ap[:, s * P:(s + 1) * P],
                                             h.ap[:, k * P:(k + 1) * P], identity[:, :])
                t = pe.done(mm)
                tiles = slice(half * per, (half + 1) * per)
                turned = bank.ap.rearrange("p (k t) -> p k t", t=P)
                act.wait(t)
                rounded = act.done(nc.scalar.activation(halves[:, 0, tiles], turned, ACT.Copy, scale=TOKEN_SCALE))
                dve.wait(rounded)
                pair.ready = [dve.done(nc.vector.scalar_tensor_tensor(
                    out=halves[:, 1, tiles], in0=turned, scalar=TOKEN_SCALE, in1=halves[:, 0, tiles],
                    op0=ALU.mult, op1=ALU.subtract))]
                bank.free = list(pair.ready)
                yield
            h.free.append(t)
            pair.free = []
            state["pair"] = pair

        def gate_product(pair, weights, weights_ready, bias, between):
            halves = as_pair(pair.ap)
            high_w, low_w = halves_of(weights)
            res = shelf.take()
            for h in range(HALVES):
                bank = product_ring.take()
                cols = slice(h * BANK, (h + 1) * BANK)
                pe.wait(pair.ready, weights_ready, bank.free)
                for t in pair_product(bank.ap,
                                      (lambda k: halves[:, 0, k, :], lambda k: halves[:, 1, k, :]),
                                      (lambda k: high_w[:, k, cols], lambda k: low_w[:, k, cols])):
                    yield
                dve.wait(t, res.free, bias.ready)
                t2 = dve.done(nc.vector.scalar_tensor_tensor(
                    out=res.ap[:, cols], in0=bank.ap, scalar=inverse["gate"][:, :],
                    in1=bias.ap[:, cols], op0=ALU.mult, op1=ALU.add))
                bank.free = [t2]
                act.wait(t2)
                res.ready = [act.done(nc.scalar.activation(res.ap[:, cols], res.ap[:, cols], ACT.Sigmoid))]
                if h == 0:
                    between()
            pair.free = [t]
            shelf.give(pair)
            weights.free = [t]
            res.free = []
            state["gate"] = res

        def gate_tiles(tiles, bias):
            n_of = dict(enumerate(tiles))
            x_bufs, pairs = {}, {}

            def prepare(n):
                buf = x_bufs[n]
                normalise(buf, buf, token_stats[:, n_of[n], :], EPS_OUTER)

            for n in range(3):
                x_bufs[n] = fetch(n_of[n], x_flat)
            for _ in range(WAIT_X):
                yield
            prepare(0)
            for _ in range(WAIT_X):
                yield
            for _ in turn_and_split(x_bufs[0]):
                yield
            shelf.give(x_bufs.pop(0))
            pairs[0] = state["pair"]
            prepare(1)
            yield TILE_DONE
            for n, tile in enumerate(tiles):
                if n + 1 < len(tiles):
                    for _ in turn_and_split(x_bufs[n + 1]):
                        yield
                    shelf.give(x_bufs.pop(n + 1))
                    pairs[n + 1] = state["pair"]
                if n + 2 < len(tiles):
                    prepare(n + 2)
                if n + 3 < len(tiles):
                    x_bufs[n + 3] = fetch(n_of[n + 3], x_flat)
                yield from gate_product(pairs.pop(n), gate_pair, gate_pair.ready, bias, lambda: None)
                res = state["gate"]
                gate_stored[tile] = store(res, gate1_dram[row_of(tile), :], res.ap)
                shelf.give(res)
                yield TILE_DONE

        def part(steps, tiles):
            for mark in steps:
                yield
                if mark is TILE_DONE:
                    tiles -= 1
                    if tiles == 0:
                        return

        def save_gate_pair():
            for k in range(KD):
                gate_pair.saved = dma(gate_pair_dram[:, k * D:(k + 1) * D], gate_pair.ap[:, k, :],
                                      dma_sem("dma_gate_pair"), gate_pair.ready)
                yield
                yield

        def fetch_params():
            dma(half_gamma[:, :], out_gamma.partition_broadcast(P), dma_sem("dma_params"))
            params = dma(half_beta[:, :], out_beta.partition_broadcast(P), dma_sem("dma_params"))
            for _ in range(SLACK):
                yield
            dve.wait(params)
            dve.done(nc.vector.tensor_scalar(half_gamma[:, :], half_gamma[:, :], 0.5, None, ALU.mult))
            pool.wait(dve.done(nc.vector.tensor_scalar(half_beta[:, :], half_beta[:, :], 0.5, None, ALU.mult)))
            yield

        def chain(*steps):
            for s in steps:
                yield from s

        state = {}
        groups = [(b, g) for g in reversed(range(NT // GROUP)) for b in range(B)]

        def tiles_of(n):
            b, g = groups[n]
            return [b * NT + g * GROUP + i for i in range(GROUP)]

        in_order = [tile for n in range(len(groups)) for tile in tiles_of(n)]
        for e in range(FIRST_PIECES, KD):
            load_piece(wide_b, wq, e)
            load_piece(wide_a, wk, e)
            if e < FIRST_PIECES + len(weight_ring.buffers):
                fetch_block()
        bias_1 = shelf.take()
        load(bias_1, bias_1.ap, gate_b.partition_broadcast(P))
        EARLY, LATE = 4, 2

        gates = gate_tiles(in_order, bias_1)

        second = load_second_fold()

        def chain_start(steps):
            next(steps)
            yield

        def stage_1():
            yield from alongside(first_fold, chain(split_gate(), chain_start(second), part(gates, 1)), RATIO_A)
            yield from alongside(part(gates, EARLY), second, 0.7)
            yield from alongside(fold(wide_b, wide_a, vo_dram, vo_stored, "vo"), chain(save_gate_pair(), fetch_params()), 0.7)
            yield from alongside(part(gates, len(in_order) - EARLY - LATE),
                                 chain(split_weights("qk", wide_a, lambda k: fetch_feature_tile(qk_dram, k, qk_stored), 2),
                                       split_weights("vo", wide_b, lambda k: fetch_feature_tile(vo_dram, k, vo_stored), 2)), 0.25)

        run(alongside(stage_1(), think_1, PACE_1))
        publish_thought()

        x1_stored, x2_stored = {}, {}

        def end_ffn_pool(xb, gb, hb, batch):
            pool.wait(gb.ready, thought_row.ready)
            t = pool.done(nc.gpsimd.tensor_tensor(gb.ap, gb.ap, thought_row.ap[:, batch, :], ALU.mult))
            gb.ready = thought_row.free = [t]
            pool.wait(xb.ready, hb.ready)
            xb.ready = [pool.done(nc.gpsimd.tensor_tensor(xb.ap, xb.ap, half_beta[:, :], ALU.add))]

        def end_ffn_sum(gb, hb):
            dve.wait(gb.ready, hb.ready, hb.free)
            gb.free = [dve.done(nc.vector.tensor_tensor(hb.ap, hb.ap, gb.ap, ALU.add))]
            st = moments(hb.ap, EPS_FFN)
            return st, one_over_std(st, st.ap[:, 4:5])

        def end_ffn_norm(xb, hb, st, t):
            dve.done(nc.vector.scalar_tensor_tensor(out=hb.ap, in0=hb.ap, scalar=st.ap[:, 0:1],
                                                    in1=half_gamma[:, :], op0=ALU.subtract, op1=ALU.mult))
            dve.wait(t, xb.ready)
            t = dve.done(nc.vector.scalar_tensor_tensor(
                out=xb.ap, in0=hb.ap, scalar=st.ap[:, 4:5], in1=xb.ap, op0=ALU.mult, op1=ALU.add))
            xb.ready, hb.free, st.free = [t], [t], [t]

        def fetch_group(n):
            for tile in tiles_of(n):
                state["xg", tile] = fetch(tile, x_flat), fetch(tile, gate1_dram, gate_stored[tile])

        def prepare_group(n):
            made = []
            for tile in tiles_of(n):
                xb, gb = state.pop(("xg", tile))
                hb = shelf.take()
                act.wait(xb.ready, hb.free)
                t = act.done(nc.scalar.activation(hb.ap, xb.ap, ACT.Identity,
                                                  bias=token_stats[:, tile, 1:2],
                                                  scale=token_stats[:, tile, 0:1]))
                hb.ready, hb.free = [t], []
                end_ffn_pool(xb, gb, hb, groups[n][0])
                yield
                yield
                end_ffn_norm(xb, hb, *end_ffn_sum(gb, hb))
                shelf.give(gb)
                yield
                x1_stored[tile] = store(xb, x1_dram[row_of(tile), :], xb.ap)
                dve.wait(xb.ready)
                st = stat_ring.take()
                pool.wait(st.free)
                t = normalisers(xb.ap, st.ap[:, 5:7], EPS_OUTER)
                for _ in range(3):
                    yield
                act.wait(t, hb.free)
                t = act.done(nc.scalar.activation(hb.ap, xb.ap, ACT.Identity,
                                                  bias=st.ap[:, 6:7], scale=st.ap[:, 5:6]))
                st.free = [t]
                hb.ready, hb.free = [t], []
                xb.free.append(t)
                shelf.give(xb)
                made.append(hb)
                yield
            state["h", n] = made

        def turn_group(n):
            keys = []
            pair = group_halves
            for i, h in enumerate(state.pop(("h", n))):
                k = shelf.take()
                for _ in turn_tile(h, k):
                    yield
                shelf.give(h)
                at = slice(i * P, (i + 1) * P)
                t = split_tile(k, pair[:, 0, :, at], pair[:, 1, :, at], group_pair.free)
                keys.append(k)
                yield
            group_pair.ready = [t]
            state["keys", n] = keys

        group_halves = group_pair.ap.rearrange("p a d -> p (a d)").bitcast(F16).rearrange(
            "p (h k t) -> p h k t", h=2, k=KD)
        high_qk, low_qk = halves_of(wide_a)
        high_vo, low_vo = halves_of(wide_b)

        def queries_and_values(n):
            q = [shelf.take() for _ in range(GROUP)]
            per_bank = BANK // (GROUP * P)
            for e0 in range(0, KD, per_bank):
                bank = product_ring.take()
                pe.wait(group_pair.ready, wide_a.ready, bank.free)
                for e in range(e0, e0 + per_bank):
                    cols = slice(e * P, (e + 1) * P)
                    part = bank.ap[:, (e - e0) * GROUP * P:(e - e0 + 1) * GROUP * P]
                    for t in pair_product(
                            part, (lambda k: high_qk[:, k, cols], lambda k: low_qk[:, k, cols]),
                            (lambda k: group_halves[:, 0, k, :], lambda k: group_halves[:, 1, k, :])):
                        pass
                    yield
                act.wait(t)
                for i in range(GROUP):
                    if e0 == 0:
                        act.wait(q[i].free)
                    src = bank.ap.rearrange("p (e g t) -> p e g t", e=per_bank, g=GROUP)[:, :, i, :]
                    t2 = act.done(nc.scalar.activation(as_features(q[i])[:, e0:e0 + per_bank, :], src, ACT.Copy,
                                                       scale=query_scale[:, :]))
                bank.free = [t2]
            wide_a.free = [t]
            for i in range(GROUP):
                q[i].ready, q[i].free = [t2], []
            v = [shelf.take() for _ in range(GROUP)]
            for i in range(GROUP):
                at = slice(i * P, (i + 1) * P)
                for h in range(HALVES):
                    bank = product_ring.take()
                    cols = slice(h * BANK, (h + 1) * BANK)
                    pe.wait(wide_b.ready, bank.free)
                    for t in pair_product(bank.ap,
                                          (lambda k: group_halves[:, 0, k, at], lambda k: group_halves[:, 1, k, at]),
                                          (lambda k: high_vo[:, k, cols], lambda k: low_vo[:, k, cols])):
                        yield
                    act.wait(t, v[i].free)
                    t2 = act.done(nc.scalar.activation(v[i].ap[:, cols], bank.ap, ACT.Copy,
                                                       scale=inverse["vo"][:, :]))
                    bank.free = [t2]
                v[i].ready, v[i].free = [t2], []
            group_pair.free = [t]
            state["qv", n] = (q, v)

        def attend(tile, q, own, before):
            x2 = state.pop(("x1", tile))
            sources = [(own, keep_own)] + ([(before, keep_prev)] if before else [])
            bank = product_ring.take()
            pe.wait(q.ready, bank.free)
            for s, ((keys, _), _) in enumerate(sources):
                pe.wait(keys.ready)
                for e in range(KD):
                    mm = nc.tensor.matmul(bank.ap[:, s * P:(s + 1) * P], as_features(keys)[:, e, :],
                                          as_features(q)[:, e, :], start=(e == 0), stop=(e == KD - 1))
                t = pe.done(mm)
                yield
            q.free.append(t)
            for (keys, _), _ in sources:
                keys.free.append(t)
            w = key_weights.take()
            dve.wait(t, w.free)
            for s, (_, keep) in enumerate(sources):
                t = dve.done(nc.vector.scalar_tensor_tensor(
                    out=w.ap[:, s, :], in0=bank.ap[:, s * P:(s + 1) * P], scalar=1.0 / TOKEN_SCALE,
                    in1=keep[:, :], op0=ALU.mult, op1=ALU.min))
            bank.free = [t]
            n = len(sources)
            t = dve.done(nc.vector.scalar_tensor_tensor(
                out=w.ap[:, 0:n, :], in0=w.ap[:, 0:n, :], scalar=0.0, in1=w.ap[:, 0:n, :],
                op0=ALU.max, op1=ALU.mult))
            state["w", tile] = (w, t, x2, sources)

        def collect(tile):
            w, weights_ready, x2, sources = state.pop(("w", tile))
            for h in range(HALVES):
                cols = slice(h * BANK, (h + 1) * BANK)
                bank = product_ring.take()
                pe.wait(weights_ready, bank.free)
                for s, ((_, values), _) in enumerate(sources):
                    pe.wait(values.ready)
                    mm = nc.tensor.matmul(bank.ap, w.ap[:, s, :], values.ap[:, cols],
                                          start=(s == 0), stop=(s == len(sources) - 1))
                t = pe.done(mm)
                dve.wait(t, x2.ready)
                t2 = dve.done(nc.vector.tensor_tensor(x2.ap[:, cols], bank.ap, x2.ap[:, cols], ALU.add))
                bank.free = [t2]
                yield
            w.free = [t]
            for (_, values), _ in sources:
                values.free.append(t)
            x2.ready = [t2]
            x2_stored[tile] = store(x2, x2_dram[row_of(tile), :], x2.ap)
            shelf.give(x2)

        def attention(n):
            waiting = state.setdefault("waiting", {})
            b, g = groups[n]
            keys, (q, v) = state.pop(("keys", n)), state.pop(("qv", n))
            t0, t1 = tiles_of(n)
            jobs = [(t1, q[1], (keys[1], v[1]), (keys[0], v[0]))]
            if b in waiting:
                tile, query, own = waiting.pop(b)
                jobs.append((tile, query, own, (keys[1], v[1])))
            if g == 0:
                jobs.append((t0, q[0], (keys[0], v[0]), None))
            else:
                waiting[b] = (t0, q[0], (keys[0], v[0]))
            for job in jobs:
                state["x1", job[0]] = fetch(job[0], x1_dram, x1_stored[job[0]])
            yield from attend(*jobs[0])
            for i, job in enumerate(jobs):
                if i + 1 < len(jobs):
                    yield from attend(*jobs[i + 1])
                yield from collect(job[0])
                shelf.give(job[1])
            for k, val in [(keys[1], v[1])] + [own for _, _, own, _ in jobs[1:]]:
                shelf.give(k, val)

        def stage_2(first, last):
            for n in range(first, last):
                more = n + 1 < len(groups)
                if more:
                    fetch_group(n + 1)
                yield from alongside(queries_and_values(n), prepare_group(n + 1) if more else iter(()), 0.75)
                yield from alongside(attention(n), turn_group(n + 1) if more else prepare_stage_3(), 1.0)

        order_3 = sorted(range(B * NT), key=lambda tile: in_order.index(tile) + 5 * (tile % GROUP == 0))
        fetched, measured, prepared, pairs_3, gates_3, sums_3 = {}, {}, {}, {}, {}, {}

        def fetch_3(n):
            if n < len(order_3):
                fetched[n] = fetch(order_3[n], x2_dram, x2_stored[order_3[n]])

        def measure_3(n):
            if n < len(order_3):
                xb = fetched[n]
                dve.wait(xb.ready)
                measured[n] = normalisers(xb.ap, token_stats[:, order_3[n], :], EPS_OUTER)

        def prepare_3(n):
            if n < len(order_3):
                xb, hb = fetched.pop(n), shelf.take()
                stats = token_stats[:, order_3[n], :]
                act.wait(measured[n], xb.ready, hb.free)
                t = act.done(nc.scalar.activation(hb.ap, xb.ap, ACT.Identity,
                                                  bias=stats[:, 1:2], scale=stats[:, 0:1]))
                hb.ready, hb.free = [t], []
                prepared[n] = xb, hb

        def turn_3(n):
            if n < len(order_3):
                yield from turn_and_split(prepared[n][1])
                pairs_3[n] = state["pair"]

        def prepare_stage_3():
            load(wide_a, wide_a.ap.rearrange("p k d -> p (k d)"), gate_pair_dram, gate_pair.saved)
            bias = state["bias"] = shelf.take()
            load(bias, bias.ap, gate_b.partition_broadcast(P))
            for n in range(4):
                fetch_3(n)
            for n in range(3):
                measure_3(n)
                yield
            for n in range(2):
                prepare_3(n)
                yield
            yield from turn_3(0)

        def sum_3(n):
            if 0 <= n < len(order_3):
                gate = gates_3.pop(n)
                sums_3[n] = end_ffn_sum(gate, prepared[n][1])
                shelf.give(gate)

        def end_3(n):
            if 0 <= n < len(order_3):
                xb, hb = prepared.pop(n)
                end_ffn_norm(xb, hb, *sums_3.pop(n))
                shelf.give(hb)
                store(xb, out_flat[row_of(order_3[n]), :], xb.ap)
                shelf.give(xb)

        def gated_3(n):
            if 0 <= n < len(order_3):
                xb, hb = prepared[n]
                end_ffn_pool(xb, gates_3[n], hb, order_3[n] // NT)

        def stage_3():
            for n in range(len(order_3)):
                sum_3(n - 2)
                yield from turn_3(n + 1)
                fetch_3(n + 4)
                gated_3(n - 1)
                prepare_3(n + 2)
                measure_3(n + 3)
                yield from gate_product(pairs_3.pop(n), wide_a, wide_a.ready, state["bias"],
                                        lambda: end_3(n - 2))
                gates_3[n] = state["gate"]
            n = len(order_3)
            gated_3(n - 1)
            for tile in (n - 2, n - 1):
                sum_3(tile)
                end_3(tile)

        fetch_group(0)
        run(alongside(part(gates, LATE), prepare_group(0), 0.8))
        run(gates)
        shelf.give(bias_1)
        dve.wait(wide_a.ready)
        act.wait(dve.done(nc.vector.tensor_scalar(query_scale[:, :], inverse["qk"][:, :], 1.0 / P, None, ALU.mult)))
        for i in range(KD):
            buf = Buffer(arena[:, i, :], dma_sem(f"dma_tile{i}"))
            buf.free = gate_pair.free + [gate_pair.saved]
            shelf.give(buf)
        run(turn_group(0))
        run(stage_2(0, B))
        last_tiles = [b * NT + NT - 1 for b in range(B)]
        think_2 = think(lambda b: x2_dram[(b + 1) * T - 1, :].rearrange("(k p) -> k p", p=P),
                        [x2_stored[t] for t in last_tiles])
        run(alongside(stage_2(B, len(groups)), think_2, PACE_2))
        publish_thought()
        run(stage_3())
        issue_stores(lambda s: True)
        sp.wait(*(Ticket(sem, n) for sem, n in dma_sems.values() if n))


_INS = ['x', 'w_attn', 'w_o', 'in_gamma', 'in_beta', 'agg_w', 'agg_b', 'pn_gamma', 'pn_beta', 'd1_w', 'd1_b',
        'd2_w', 'd2_b', 'bc_w', 'bc_b', 'gate_w', 'gate_b', 'out_gamma', 'out_beta']


def kernel(**inputs):
    import numpy as _np
    import concourse.bacc as _bacc
    from concourse import mybir as _mybir
    from concourse.bass_utils import run_bass_kernel_spmd as _run

    nc = _bacc.Bacc("TRN2", target_bir_lowering=False, num_devices=1)
    arrays, args = {}, []
    for name in _INS:
        full = ("L0_attn_" if name in ("x", "w_attn", "w_o") else "L0_ffn_") + name
        a = _np.ascontiguousarray(inputs[full])
        arrays[f"in_{name}"] = a
        args.append(nc.dram_tensor(f"in_{name}", a.shape, _mybir.dt.from_np(a.dtype), kind="ExternalInput").ap())
    shape = inputs["L0_attn_x"].shape
    args.append(nc.dram_tensor("out_0", shape, _mybir.dt.float32, kind="ExternalOutput").ap())
    macaron_kernel(nc, *args)
    r = _run(nc, [arrays], core_ids=[0])
    return r.results[0]["out_0"]
```

```python
from contextlib import ExitStack
from itertools import accumulate

import concourse.bass as bass
from concourse import mybir

F32 = mybir.dt.float32
F16 = mybir.dt.float16
BF16 = mybir.dt.bfloat16
I32 = mybir.dt.int32
ALU = mybir.AluOpType
ACT = mybir.ActivationFunctionType
AX_X = mybir.AxisListType.X

P = 128
BANK = 512
PE_COLS = 32
K_STEPS = 4
TILE_DONE = "tile done"
SLACK = 2
STORE_DELAY = 6
GATE_WAIT = 3
TOKEN_WAIT = 2
FOLD_SPLIT_PACE = 0.6
GATE_FETCH_PACE = 0.7
FOLD_SAVE_PACE = 0.7
GATE_SPLIT_PACE = 0.25
GATE_GROUP_PACE = 0.8
VALUES_GROUP_PACE = 0.9
ATTENTION_TURN_PACE = 1.0
PACE_1 = 0.6
PACE_2 = 0.65
EPS_OUTER = 1e-5
EPS_FFN = 1e-6
TOKEN_SCALE = 1024.0
QUERY_SCALE = 2.0 ** -20
EXPONENT_BITS = 0x7F800000
WEIGHT_TOP = 8192.0
TINY = 2.0 ** -100
NEVER = 3.0e38


class Ticket:

    def __init__(self, sem, value):
        self.sem, self.value = sem, value


class Stream:

    def __init__(self, eng, sem, serial):
        self.eng, self.sem, self.count, self.serial, self.seen = eng, sem, 0, serial, {}

    def wait(self, *tickets):
        for t in tickets:
            if isinstance(t, (list, tuple)):
                self.wait(*t)
            elif t is not None and self.seen.get(t.sem.name, 0) < t.value:
                self.eng.wait_ge(t.sem, t.value)
                self.seen[t.sem.name] = t.value

    def done(self, instruction):
        instruction.then_inc(self.sem, 1)
        self.count += 1
        t = Ticket(self.sem, self.count)
        if self.serial:
            self.wait(t)
        return t

    def last(self):
        return Ticket(self.sem, self.count) if self.count else None


class Buffer:

    def __init__(self, ap, dma_sem=None):
        self.ap, self.dma_sem, self.dma_count = ap, dma_sem, 0
        self.ready, self.free = [], []


class Ring:
    def __init__(self, buffers):
        self.buffers, self.at = buffers, 0

    def take(self):
        self.at += 1
        return self.buffers[(self.at - 1) % len(self.buffers)]


class Shelf:

    def __init__(self, buffers):
        self.free = list(buffers)

    def take(self):
        return self.free.pop(0)

    def give(self, *buffers):
        self.free.extend(buffers)


def macaron_kernel(nc, x, w_attn, w_o, in_gamma, in_beta, agg_w, agg_b, pn_gamma, pn_beta,
                   d1_w, d1_b, d2_w, d2_b, bc_w, bc_b, gate_w, gate_b, out_gamma, out_beta, out):
    B, T, D = x.shape
    H = d1_w.shape[1]
    KD, KH = D // P, H // P
    NT = T // P
    HALVES = D // BANK
    GROUP = 2
    WCHUNK = 2 * D
    assert B == 2 and D == 1024 and H % WCHUNK == 0 and NT % GROUP == 0

    x_flat, out_flat = (a.rearrange("b t d -> (b t) d") for a in (x, out))
    row_of = lambda tile: slice(tile * P, (tile + 1) * P)
    gate1_dram = nc.dram_tensor("gate1_scratch", [B * T, D], F32, kind="Internal").ap()
    x1_dram = nc.dram_tensor("x1_scratch", [B * T, D], F32, kind="Internal").ap()
    x2_dram = nc.dram_tensor("x2_scratch", [B * T, D], F32, kind="Internal").ap()
    qk_dram = nc.dram_tensor("qk_scratch", [D, D], F32, kind="Internal").ap()
    vo_dram = nc.dram_tensor("vo_scratch", [D, D], F32, kind="Internal").ap()
    gate_pair_dram = nc.dram_tensor("gate_pair_scratch", [P, KD * D], F32, kind="Internal").ap()
    row_dram = nc.dram_tensor("row_scratch", [B * KD, P], F32, kind="Internal").ap()

    whole = ExitStack()
    with whole:
        def new_sem(name):
            return whole.enter_context(nc.semaphore(name))

        pe = Stream(nc.tensor, new_sem("pe_done"), serial=False)
        act = Stream(nc.scalar, new_sem("act_done"), serial=True)
        dve = Stream(nc.vector, new_sem("dve_done"), serial=True)
        pool = Stream(nc.gpsimd, new_sem("pool_done"), serial=True)
        sp = Stream(nc.sync, new_sem("sp_done"), serial=False)

        def sbuf(stack, name, shape, dtype=F32):
            return stack.enter_context(nc.sbuf_tensor(name, shape, dtype))

        dma_sems = {}

        def dma_sem(name):
            if name not in dma_sems:
                dma_sems[name] = [new_sem(name), 0]
            return dma_sems[name]

        late_stores = []
        steps_made = [0]

        def issue_stores(up_to):
            while late_stores and up_to(late_stores[0]):
                late_stores.pop(0)[1]()

        def tick():
            steps_made[0] += 1
            issue_stores(lambda s: s[2] <= steps_made[0])

        def flat(tickets):
            for t in tickets:
                if isinstance(t, (list, tuple)):
                    yield from flat(t)
                elif t is not None:
                    yield t

        def dma(to, source, sem, *waits):
            for t in flat(waits):
                while any(t is s[0] for s in late_stores):
                    late_stores.pop(0)[1]()
            sp.wait(*waits)
            nc.sync.dma_start(to, source).then_inc(sem[0], 16)
            sem[1] += 16
            return Ticket(sem[0], sem[1])

        def buffers(stack, name, n, shape, dtype=F32):
            return [Buffer(sbuf(stack, f"{name}{i}", shape, dtype), dma_sem(f"dma_{name}{i}"))
                    for i in range(n)]

        def as_pair(ap):
            return ap.bitcast(F16).rearrange("p (h k t) -> p h k t", h=2, k=KD)

        def load(buf, to, source, *waits):
            buf.ready = [dma(to, source, buf.dma_sem, buf.free, *waits)]
            buf.free = []

        def store(buf, to, source):
            sem, ready = buf.dma_sem, buf.ready
            sem[1] += 16
            t = Ticket(sem[0], sem[1])

            def issue():
                sp.wait(ready)
                nc.sync.dma_start(to, source).then_inc(sem[0], 16)

            late_stores.append((t, issue, steps_made[0] + STORE_DELAY))
            buf.free.append(t)
            return t

        product_banks = whole.enter_context(nc.psum_tensor("product_banks", [P, 4, BANK], F32))
        turn_banks = whole.enter_context(nc.psum_tensor("turn_banks", [P, 2, BANK], F32))
        thought_acc = Buffer(whole.enter_context(nc.psum_tensor("thought_acc", [P, BANK], F32))[:, :])
        thought_turn = Buffer(whole.enter_context(nc.psum_tensor("thought_turn", [P, BANK], F32))[:, :])
        product_ring = Ring([Buffer(product_banks[:, i, :]) for i in range(4)])
        turn_ring = Ring([Buffer(turn_banks[:, i, :]) for i in range(2)])

        identity = sbuf(whole, "identity", [P, P])
        mean_maker = sbuf(whole, "mean_maker", [P, P])
        keep_prev = sbuf(whole, "keep_prev", [P, P], BF16)
        keep_own = sbuf(whole, "keep_own", [P, P], BF16)
        minus_half = sbuf(whole, "minus_half", [P, 2])
        half_gamma = sbuf(whole, "half_gamma", [P, D])
        half_beta = sbuf(whole, "half_beta", [P, D])
        thought_row = Buffer(sbuf(whole, "thought_row", [P, B, D]), dma_sem("dma_thought_row"))
        token_stats = sbuf(whole, "token_stats", [P, B * NT, 2])
        bn_parts = sbuf(whole, "bn_parts", [P, HALVES, 6])
        weight_ring = Ring(buffers(whole, "thought_weights", 3, [P, WCHUNK]))
        wide_a = Buffer(sbuf(whole, "wide_a", [P, KD, D]), dma_sem("dma_wide_a"))
        wide_b = Buffer(sbuf(whole, "wide_b", [P, KD, D]), dma_sem("dma_wide_b"))
        thought = sbuf(whole, "thought", [P, B, KD])
        centred = sbuf(whole, "centred", [P, B, KD])
        squares = sbuf(whole, "squares", [P, B, KD])
        t_small = sbuf(whole, "t_small", [P, 3, B])
        hidden = sbuf(whole, "hidden", [P, B, KH])
        spread = sbuf(whole, "spread", [P, B, KD])
        narrow_in = sbuf(whole, "narrow_in", [P, KD, B])
        narrow_hidden = sbuf(whole, "narrow_hidden", [P, KH, B])
        t_wide = Buffer(sbuf(whole, "t_wide", [P, BANK]))
        t_rows = t_wide.ap[:, 0:P]
        vectors = sbuf(whole, "vectors", [P, P])
        d1_bias = sbuf(whole, "d1_bias", [P, KH])
        scale_stat = {m: sbuf(whole, f"scale_stat_{m}", [P, KD + 3]) for m in ("gate", "qk", "vo")}
        key_weights = Shelf(buffers(whole, "key_weights", 5, [P, 2, P]))
        score_scale = sbuf(whole, "score_scale", [P, 1])
        stat_ring = Ring([Buffer(sbuf(whole, f"stats{i}", [P, 8])[:, :]) for i in range(4)])
        TILES = 23
        arena = sbuf(whole, "arena", [P, TILES, D])
        gate_pair = Buffer(arena[:, 0:KD, :])
        group_ring = Ring([Buffer(arena[:, i:i + GROUP, :]) for i in (TILES - 2 * GROUP, TILES - GROUP)])
        halves_in_arena = arena[:, :, :].rearrange("p i d -> p (i d)").bitcast(F16).rearrange(
            "p (i h k t) -> p i h k t", h=2, k=KD, t=P)

        def tile_buffer(i):
            buf = Buffer(arena[:, i, :], dma_sem(f"dma_tile{i}"))
            buf.slot = i
            return buf

        QUERY_TILES = B + GROUP + 1
        query_shelf = Shelf([])
        shelf = Shelf([tile_buffer(i) for i in range(KD, TILES - 2 * GROUP)])
        inverse = {m: sbuf(whole, f"inverse_{m}", [P, 1]) for m in ("gate", "qk", "vo")}

        def load_piece(buf, source, e):
            if e == 0:
                buf.piece_ready = []
            buf.piece_ready.append(dma(buf.ap[:, e, :], source[e * P:(e + 1) * P, :],
                                       dma_sem(f"{buf.name}_piece{e}"), buf.free))

        def fold(left, right, dest_dram, stored, matrix):
            sizes = [2] + [1] * (KD - 2)
            for d0, size in zip(accumulate([0] + sizes), sizes):
                banks = [product_ring.take() for _ in range(size * HALVES)]
                pe.wait(*(bank.free for bank in banks))
                for e in range(KD):
                    pe.wait(left.piece_ready[e], right.piece_ready[e])
                    for n, bank in enumerate(banks):
                        d, h = d0 + n // HALVES, n % HALVES
                        mm = nc.tensor.matmul(bank.ap, left.ap[:, e, d * P:(d + 1) * P],
                                              right.ap[:, e, h * BANK:(h + 1) * BANK],
                                              start=(e == 0), stop=(e == KD - 1))
                        if n == 1 and size > 1:
                            yield
                    t = pe.done(mm)
                    yield
                for i in range(size):
                    res = shelf.take()
                    act.wait(t, res.free)
                    for h in range(HALVES):
                        t2 = act.done(nc.scalar.copy(res.ap[:, h * BANK:(h + 1) * BANK],
                                                     banks[i * HALVES + h].ap))
                        banks[i * HALVES + h].free = [t2]
                    res.ready, res.free = [t2], []
                    d = d0 + i
                    note_largest(res, matrix, d)
                    stored.append(store(res, dest_dram[d * P:(d + 1) * P, :], res.ap))
                    shelf.give(res)
            left.free, right.free = [t], [t]

        def note_largest(buf, matrix, k):
            dve.wait(buf.ready)
            t = dve.done(nc.vector.tensor_reduce(scale_stat[matrix][:, k:k + 1], buf.ap, AX_X, ALU.max,
                                                 apply_absolute_value=True))
            buf.free.append(t)

        pool.done(nc.gpsimd.memset(identity[:, :], 0.0))
        pool.done(nc.gpsimd.affine_select(out=identity[:, :], in_=identity[:, :], compare_op=ALU.not_equal,
                                          fill=1.0, base=0, pattern=[[-1, P]], channel_multiplier=1))
        for keep in (keep_prev, keep_own):
            pool.done(nc.gpsimd.memset(keep[:, :], NEVER))
        pool.done(nc.gpsimd.affine_select(out=keep_prev[:, :], in_=keep_prev[:, :], compare_op=ALU.is_ge,
                                          fill=0.0, base=0, pattern=[[-1, P]], channel_multiplier=1))
        constants = pool.done(nc.gpsimd.affine_select(
            out=keep_own[:, :], in_=keep_own[:, :], compare_op=ALU.is_ge,
            fill=0.0, base=0, pattern=[[1, P]], channel_multiplier=-1))
        dve.done(nc.vector.memset(mean_maker[:, :], 1.0 / D))
        dve.done(nc.vector.memset(minus_half[:, :], -0.5))
        dve.done(nc.vector.memset(thought_acc.ap, 0.0))
        zeroed = dve.done(nc.vector.memset(t_wide.ap[:, :], 0.0))
        wq, wk, wv = (w_attn[i * D:(i + 1) * D, :] for i in range(3))
        FIRST_PIECES = 2
        wide_a.name, wide_b.name = "wide_a", "wide_b"
        for e in range(FIRST_PIECES):
            load_piece(wide_b, wq, e)
            load_piece(wide_a, wk, e)

        qk_stored, vo_stored, gate_stored = [], [], {}
        first_fold = fold(wide_b, wide_a, qk_dram, qk_stored, "qk")
        for _ in range(2 * FIRST_PIECES):
            next(first_fold)
        pe.wait(constants, zeroed)

        VECTOR_ROWS, BIAS_ROWS, THOUGHT_ROWS = range(3)

        def turn_rows(rows_ready, block, dest, n):
            pe.wait(rows_ready, thought_turn.free)
            t = pe.done(nc.tensor.transpose(thought_turn.ap[:, 0:P], t_wide.ap[:, block * P:(block + 1) * P],
                                            identity[:, :]))
            t_wide.free = [t]
            dve.wait(t)
            t = dve.done(nc.vector.tensor_copy(dest, thought_turn.ap[:, 0:n]))
            thought_turn.free = [t]
            return t

        names = (in_gamma, in_beta, agg_b, pn_gamma, pn_beta, d2_b, bc_b)
        sp.wait(zeroed)
        for v, vec in enumerate(names):
            for b in range(B):
                at = (v * B + b) * KD
                rows = dma(t_rows[at:at + KD, :], vec.rearrange("(k p) -> k p", p=P),
                           dma_sem("dma_vectors"))
        bias_rows = dma(t_wide.ap[0:KH, BIAS_ROWS * P:(BIAS_ROWS + 1) * P], d1_b.rearrange("(k p) -> k p", p=P),
                        dma_sem("dma_d1_bias"))
        V_IN_G, V_IN_B, V_AGG_B, V_PN_G, V_PN_B, V_D2_B, V_BC_B = range(len(names))
        vector_of = lambda v, b: vectors[:, (v * B + b) * KD:(v * B + b + 1) * KD]

        def weight_blocks():
            def narrow(w, tiles):
                for k in range(0, tiles, 2):
                    yield w[k * P:(k + 2) * P, :].rearrange("(k p) n -> p k n", p=P)

            def wide(w):
                for c in range(H // WCHUNK):
                    for k in range(KD):
                        yield w[k * P:(k + 1) * P, c * WCHUNK:(c + 1) * WCHUNK]

            for _ in range(2):
                yield from narrow(agg_w, KD)
                for _ in range(K_STEPS):
                    yield from wide(d1_w)
                    yield from narrow(d2_w, KH)
                yield from narrow(bc_w, KD)

        blocks = weight_blocks()
        pending = []

        def fetch_block():
            source = next(blocks, None)
            if source is not None:
                buf = weight_ring.take()
                to = buf.ap[:, :]
                if len(source.shape) == 3:
                    to = to.rearrange("p (k n) -> p k n", k=2)
                load(buf, to, source)
                pending.append(buf)

        def next_block():
            return pending.pop(0)

        def used_block(buf, t):
            buf.free = [t]
            fetch_block()

        def slack():
            for _ in range(SLACK):
                yield

        def norm_thought(source, dest, eps, ready, gamma=None, beta=None):
            pe.wait(ready, thought_turn.free)
            t = pe.done(nc.tensor.matmul(thought_turn.ap[:, 0:B * KD], mean_maker[:, :],
                                         source[:, :, :].rearrange("p b k -> p (b k)"), start=True, stop=True))
            sums = thought_turn.ap[:, 0:B * KD].rearrange("p (b k) -> p b k", b=B)
            dve.wait(t)
            dve.done(nc.vector.tensor_reduce(t_small[:, 0, :], sums, AX_X, ALU.add))
            for b in range(B):
                dve.done(nc.vector.tensor_scalar(centred[:, b, :], source[:, b, :], t_small[:, 0, b:b + 1],
                                                 None, ALU.subtract))
            t = dve.done(nc.vector.tensor_tensor(squares[:, :, :], centred[:, :, :], centred[:, :, :], ALU.mult))
            yield from slack()
            pe.wait(t)
            t = pe.done(nc.tensor.matmul(thought_turn.ap[:, 0:B * KD], mean_maker[:, :],
                                         squares[:, :, :].rearrange("p b k -> p (b k)"), start=True, stop=True))
            dve.wait(t)
            t = dve.done(nc.vector.tensor_reduce(t_small[:, 1, :], sums, AX_X, ALU.add))
            thought_turn.free = [t]
            t = dve.done(nc.vector.tensor_scalar(t_small[:, 1, :], t_small[:, 1, :], eps, None, ALU.add))
            pool.wait(t)
            t = pool.done(nc.gpsimd.tensor_tensor(t_small[:, 2, :], t_small[:, 1, :], minus_half[:, 0:B], ALU.pow))
            dve.wait(t)
            for b in range(B):
                scaled = centred[:, b, :] if gamma is not None else dest(b)
                if gamma is None:
                    t = dve.done(nc.vector.tensor_scalar(dest(b), centred[:, b, :], t_small[:, 2, b:b + 1],
                                                         None, ALU.mult))
                else:
                    dve.done(nc.vector.scalar_tensor_tensor(
                        out=scaled, in0=centred[:, b, :], scalar=t_small[:, 2, b:b + 1],
                        in1=vector_of(gamma, b), op0=ALU.mult, op1=ALU.mult))
                    t = dve.done(nc.vector.tensor_tensor(dest(b), scaled, vector_of(beta, b), ALU.add))
            yield from slack()
            yield t

        def turn_sums(t):
            dve.wait(t, t_wide.free)
            t = dve.done(nc.vector.tensor_copy(t_wide.ap[:, :], thought_acc.ap[:, :]))
            thought_acc.free = [t]
            yield from slack()
            pe.wait(t, thought_turn.free)
            for s in range(BANK // P):
                mm = nc.tensor.transpose(thought_turn.ap[:, s * P:(s + 1) * P],
                                         t_wide.ap[:, s * P:(s + 1) * P], identity[:, :])
            t = pe.done(mm)
            t_wide.free = [t]
            yield t

        def turned_view(j, b):
            return thought_turn.ap.rearrange("p (s r) -> p s r", r=P)[:, :, PE_COLS * j + b]

        def narrow_product(stationary, tiles, ready, finish):
            pe.wait(ready, thought_acc.free)
            for i in range(0, tiles, 2):
                buf = next_block()
                pe.wait(buf.ready)
                w = buf.ap[:, :].rearrange("p (k n) -> p k n", k=2)
                for a in range(2):
                    for h in range(HALVES):
                        j = 2 * a + h
                        mm = nc.tensor.matmul(thought_acc.ap[PE_COLS * j:PE_COLS * j + B, :],
                                              stationary[:, i + a, :], w[:, a, h * BANK:(h + 1) * BANK],
                                              start=(i == 0), stop=(i == tiles - 2))
                t = pe.done(mm)
                used_block(buf, t)
                yield
            for t in turn_sums(t):
                yield
            dve.wait(t)
            per = BANK // P
            for b in range(B):
                for h in range(HALVES):
                    both = thought_turn.ap.rearrange("p (s a r) -> p s a r", a=2, r=2 * PE_COLS)[
                        :, :, :, PE_COLS * h + b]
                    t = dve.done(nc.vector.tensor_reduce(squares[:, b, h * per:(h + 1) * per], both, AX_X, ALU.add))
            thought_turn.free = [t]
            finish()
            yield from slack()

        def add_bias(bias, dest):
            def go():
                for b in range(B):
                    dve.done(nc.vector.tensor_tensor(dest[:, b, :], squares[:, b, :], vector_of(bias, b), ALU.add))
            return go

        def add_step():
            add_bias(V_D2_B, squares)()
            dve.done(nc.vector.tensor_tensor(thought[:, :, :], thought[:, :, :], squares[:, :, :], ALU.add))

        def wide_product(ready):
            for c in range(H // WCHUNK):
                pe.wait(ready, thought_acc.free)
                for k in range(KD):
                    buf = next_block()
                    pe.wait(buf.ready)
                    for j in range(WCHUNK // BANK):
                        mm = nc.tensor.matmul(thought_acc.ap[PE_COLS * j:PE_COLS * j + B, :],
                                              narrow_in[:, k, :], buf.ap[:, j * BANK:(j + 1) * BANK],
                                              start=(k == 0), stop=(k == KD - 1))
                    t = pe.done(mm)
                    used_block(buf, t)
                    yield
                for t in turn_sums(t):
                    yield
                dve.wait(t)
                per = BANK // P
                for b in range(B):
                    for j in range(WCHUNK // BANK):
                        at = (c * (WCHUNK // BANK) + j) * per
                        t = dve.done(nc.vector.tensor_tensor(hidden[:, b, at:at + per], turned_view(j, b),
                                                             d1_bias[:, at:at + per], ALU.add))
                thought_turn.free = [t]
            act.wait(t, pe.last())
            for b in range(B):
                t = act.done(nc.scalar.activation(narrow_hidden[:, :, b], hidden[:, b, :], ACT.Gelu))
            yield from slack()
            yield t

        def think(source_rows, ready):
            for b in range(B):
                rows = dma(t_wide.ap[b * KD:(b + 1) * KD, THOUGHT_ROWS * P:(THOUGHT_ROWS + 1) * P],
                           source_rows(b), dma_sem("dma_thought_in"), ready, t_wide.free)
            yield
            t = turn_rows(rows, THOUGHT_ROWS, thought[:, :, :].rearrange("p b k -> p (b k)"), B * KD)
            yield
            into_thought = lambda b: thought[:, b, :]
            into_narrow = lambda b: narrow_in[:, :, b]
            for t in norm_thought(thought, into_thought, EPS_OUTER, t):
                yield
            for t in norm_thought(thought, into_narrow, EPS_FFN, t, V_IN_G, V_IN_B):
                yield
            yield from narrow_product(narrow_in, KD, t, add_bias(V_AGG_B, thought))
            for _ in range(K_STEPS):
                for t in norm_thought(thought, into_narrow, EPS_FFN, dve.last(), V_PN_G, V_PN_B):
                    yield
                for t in wide_product(t):
                    yield
                yield from narrow_product(narrow_hidden, KH, t, add_step)
            for b in range(B):
                t = dve.done(nc.vector.tensor_copy(narrow_in[:, :, b], thought[:, b, :]))
            yield from narrow_product(narrow_in, KD, t, add_bias(V_BC_B, spread))
            pe.wait(dve.last(), thought_turn.free)
            t = pe.done(nc.tensor.matmul(thought_turn.ap[0:B * KD, 0:P], spread[:, :, :].rearrange("p b k -> p (b k)"),
                                         identity[:, :], start=True, stop=True))
            dve.wait(t, t_wide.free)
            t = dve.done(nc.vector.tensor_copy(t_rows[0:B * KD, :], thought_turn.ap[0:B * KD, 0:P]))
            thought_turn.free = [t]
            t_wide.free = [dma(row_dram, t_rows[0:B * KD, :], dma_sem("dma_row_scratch"), t)]

        def publish_thought():
            load(thought_row, thought_row.ap[:, :, :].rearrange("p b d -> p (b d)"),
                 row_dram.rearrange("k p -> (k p)").partition_broadcast(P), t_wide.free)

        def moments(source, eps):
            st = stat_ring.take()
            dve.wait(st.free)
            for h in range(HALVES):
                dve.done(nc.vector.bn_stats(bn_parts[:, h, :], source[:, h * BANK:(h + 1) * BANK]))
            dve.done(nc.vector.bn_aggr(st.ap[:, 0:2], bn_parts[:, :, :]))
            t = dve.done(nc.vector.tensor_scalar(st.ap[:, 2:3], st.ap[:, 1:2], eps, None, ALU.add))
            st.ready, st.free = [t], []
            return st

        def one_over_std(st, dest):
            pool.wait(st.ready)
            return pool.done(nc.gpsimd.tensor_tensor(dest, st.ap[:, 2:3], minus_half[:, 0:1], ALU.pow))

        def normalisers(source, dest, eps):
            st = moments(source, eps)
            t = dve.done(nc.vector.tensor_scalar(st.ap[:, 3:4], st.ap[:, 0:1], -1.0, None, ALU.mult))
            one_over_std(st, dest[:, 0:1])
            pool.wait(t)
            t = pool.done(nc.gpsimd.tensor_tensor(dest[:, 1:2], st.ap[:, 3:4], dest[:, 0:1], ALU.mult))
            st.free = [t]
            return t

        def turn_tile(h, high, low, pair_free):
            per = BANK // P
            act.wait(pair_free)
            for half in range(HALVES):
                bank = turn_ring.take()
                pe.wait(h.ready, bank.free)
                for s in range(per):
                    k = half * per + s
                    mm = nc.tensor.transpose(bank.ap[:, s * P:(s + 1) * P],
                                             h.ap[:, k * P:(k + 1) * P], identity[:, :])
                t = pe.done(mm)
                tiles = slice(half * per, (half + 1) * per)
                turned = bank.ap.rearrange("p (k t) -> p k t", t=P)
                act.wait(t)
                rounded = act.done(nc.scalar.activation(high[:, tiles], turned, ACT.Copy, scale=TOKEN_SCALE))
                dve.wait(rounded)
                made = dve.done(nc.vector.scalar_tensor_tensor(
                    out=low[:, tiles], in0=turned, scalar=TOKEN_SCALE, in1=high[:, tiles],
                    op0=ALU.mult, op1=ALU.subtract))
                bank.free = [made]
                if half == HALVES - 1:
                    h.free.append(t)
                yield made

        def pair_product(bank, left, right):
            n = 0
            for k in range(KD):
                for a, b in ((0, 0), (0, 1), (1, 0)):
                    mm = nc.tensor.matmul(bank, left[a](k), right[b](k), start=(n == 0), stop=(n == 3 * KD - 1))
                    n += 1
                    if n == 3 * KD:
                        yield pe.done(mm)
                    elif n % KD == 0:
                        yield

        def split_weights(matrix, wide, fetch_rows, ahead):
            high, low = halves_of(wide)
            rows = [fetch_rows(k) for k in range(ahead)]
            stat = scale_stat[matrix]
            top, exponent, scale = (stat[:, KD + i:KD + i + 1] for i in range(3))
            t = dve.done(nc.vector.tensor_reduce(top, stat[:, 0:KD], AX_X, ALU.max))
            pool.wait(t)
            t = pool.done(nc.gpsimd.partition_all_reduce(exponent, top, P, bass.bass_isa.ReduceOp.max))
            for _ in range(2):
                yield
            dve.wait(t)
            dve.done(nc.vector.tensor_scalar(top, exponent, TINY, None, ALU.max))
            dve.done(nc.vector.tensor_scalar(exponent.bitcast(I32), top.bitcast(I32), EXPONENT_BITS, None,
                                             ALU.bitwise_and))
            dve.done(nc.vector.tensor_scalar(scale.bitcast(I32), top.bitcast(I32), EXPONENT_BITS, EXPONENT_BITS,
                                             ALU.bitwise_and, ALU.bitwise_xor))
            dve.done(nc.vector.tensor_scalar(scale, scale, WEIGHT_TOP, None, ALU.mult))
            dve.done(nc.vector.tensor_scalar(inverse[matrix][:, :], exponent,
                                             1.0 / (2.0 * WEIGHT_TOP * TOKEN_SCALE), None, ALU.mult))
            dve.wait(wide.free)
            for k in range(KD):
                yield
                buf = rows.pop(0)
                dve.wait(buf.ready)
                dve.done(nc.vector.tensor_scalar(high[:, k, :], buf.ap, scale, None, ALU.mult))
                t = dve.done(nc.vector.scalar_tensor_tensor(out=low[:, k, :], in0=buf.ap, scalar=scale,
                                                            in1=high[:, k, :], op0=ALU.mult, op1=ALU.subtract))
                buf.free.append(t)
                shelf.give(buf)
                if k + ahead < KD:
                    rows.append(fetch_rows(k + ahead))
            wide.ready, wide.free = [t], []
            yield

        def split_gate():
            rows = [fetch_feature_tile(gate_w, k) for k in range(KD)]
            for _ in range(GATE_WAIT):
                yield
            for k in range(KD):
                yield
                note_largest(rows[k], "gate", k)
            yield from split_weights("gate", gate_pair, lambda k: rows[k], KD)

        def fetch_feature_tile(source, k, *waits):
            buf = shelf.take()
            load(buf, buf.ap, source[k * P:(k + 1) * P, :], *waits)
            return buf

        def halves_of(wide):
            v = wide.ap[:, :, :].rearrange("p k d -> p (k d)").bitcast(F16).rearrange(
                "p (h k d) -> p h k d", h=2, k=KD)
            return v[:, 0], v[:, 1]

        def alongside(main, other, pace):
            due = 0.0
            for _ in main:
                tick()
                yield
                due += pace
                while due >= 1.0:
                    due -= 1.0
                    next(other, None)
            for _ in other:
                tick()
                yield

        def run(steps):
            for _ in steps:
                tick()

        think_1 = think(lambda b: x[b, T - 1, :].rearrange("(k p) -> k p", p=P), None)
        next(think_1)
        turn_rows(rows, VECTOR_ROWS, vectors[:, 0:len(names) * B * KD], len(names) * B * KD)
        turn_rows(bias_rows, BIAS_ROWS, d1_bias[:, :], KH)


        def load_second_fold():
            per, ahead = BANK // P, 3
            rows = []

            def fetch_rows(n):
                if n < KD:
                    buf = shelf.take()
                    load(buf, buf.ap, w_o[n * P:(n + 1) * P, :])
                    rows.append(buf)

            for n in range(ahead):
                fetch_rows(n)
            yield
            for n in range(KD):
                fetch_rows(n + ahead)
                load_piece(wide_b, wv, n)
                buf = rows.pop(0)
                for h in range(HALVES):
                    bank = turn_ring.take()
                    pe.wait(buf.ready, bank.free)
                    for s in range(per):
                        e = h * per + s
                        mm = nc.tensor.transpose(bank.ap[:, s * P:(s + 1) * P],
                                                 buf.ap[:, e * P:(e + 1) * P], identity[:, :])
                    t = pe.done(mm)
                    act.wait(t, wide_a.free)
                    t2 = act.done(nc.scalar.copy(wide_a.ap[:, h * per:(h + 1) * per, n * P:(n + 1) * P],
                                                 bank.ap.rearrange("p (k t) -> p k t", t=P)))
                    bank.free = [t2]
                    yield
                buf.free = [t]
                shelf.give(buf)
            wide_a.piece_ready = [t2] * KD

        def fetch(tile, source, *waits):
            buf = shelf.take()
            load(buf, buf.ap, source[row_of(tile), :], *waits)
            return buf

        def normalise(source, dest, stats, eps):
            dve.wait(source.ready)
            t = normalisers(source.ap, stats, eps)
            act.wait(t, source.ready, dest.free)
            t = act.done(nc.scalar.activation(dest.ap, source.ap, ACT.Identity,
                                              bias=stats[:, 1:2], scale=stats[:, 0:1]))
            dest.ready, dest.free = [t], []
            return t

        def turn_and_split(h):
            pair = shelf.take()
            halves = as_pair(pair.ap)
            for t in turn_tile(h, halves[:, 0], halves[:, 1], pair.free):
                pair.ready = [t]
                yield
            pair.free = []
            state["pair"] = pair

        def gate_product(pair, weights, weights_ready, bias, between):
            halves = as_pair(pair.ap)
            high_w, low_w = halves_of(weights)
            res = shelf.take()
            for h in range(HALVES):
                bank = product_ring.take()
                cols = slice(h * BANK, (h + 1) * BANK)
                pe.wait(pair.ready, weights_ready, bank.free)
                for t in pair_product(bank.ap,
                                      (lambda k: halves[:, 0, k, :], lambda k: halves[:, 1, k, :]),
                                      (lambda k: high_w[:, k, cols], lambda k: low_w[:, k, cols])):
                    yield
                dve.wait(t, res.free, bias.ready)
                t2 = dve.done(nc.vector.scalar_tensor_tensor(
                    out=res.ap[:, cols], in0=bank.ap, scalar=inverse["gate"][:, :],
                    in1=bias.ap[:, cols], op0=ALU.mult, op1=ALU.add))
                bank.free = [t2]
                act.wait(t2)
                res.ready = [act.done(nc.scalar.activation(res.ap[:, cols], res.ap[:, cols], ACT.Sigmoid))]
                if h == 0:
                    between()
            pair.free = [t]
            shelf.give(pair)
            weights.free = [t]
            res.free = []
            state["gate"] = res

        def gate_tiles(tiles, bias):
            n_of = dict(enumerate(tiles))
            x_bufs, pairs = {}, {}

            def prepare(n):
                buf = x_bufs[n]
                normalise(buf, buf, token_stats[:, n_of[n], :], EPS_OUTER)

            for n in range(3):
                x_bufs[n] = fetch(n_of[n], x_flat)
            for _ in range(TOKEN_WAIT):
                yield
            prepare(0)
            for _ in range(TOKEN_WAIT):
                yield
            for _ in turn_and_split(x_bufs[0]):
                yield
            shelf.give(x_bufs.pop(0))
            pairs[0] = state["pair"]
            prepare(1)
            yield TILE_DONE
            for n, tile in enumerate(tiles):
                if n + 1 < len(tiles):
                    for _ in turn_and_split(x_bufs[n + 1]):
                        yield
                    shelf.give(x_bufs.pop(n + 1))
                    pairs[n + 1] = state["pair"]
                if n + 2 < len(tiles):
                    prepare(n + 2)
                if n + 3 < len(tiles):
                    x_bufs[n + 3] = fetch(n_of[n + 3], x_flat)
                yield from gate_product(pairs.pop(n), gate_pair, gate_pair.ready, bias, lambda: None)
                res = state["gate"]
                gate_stored[tile] = store(res, gate1_dram[row_of(tile), :], res.ap)
                shelf.give(res)
                yield TILE_DONE

        def part(steps, tiles):
            for mark in steps:
                yield
                if mark is TILE_DONE:
                    tiles -= 1
                    if tiles == 0:
                        return

        def save_gate_pair():
            for k in range(KD):
                gate_pair.saved = dma(gate_pair_dram[:, k * D:(k + 1) * D], gate_pair.ap[:, k, :],
                                      dma_sem("dma_gate_pair"), gate_pair.ready)
                yield
                yield

        def fetch_params():
            dma(half_gamma[:, :], out_gamma.partition_broadcast(P), dma_sem("dma_params"))
            params = dma(half_beta[:, :], out_beta.partition_broadcast(P), dma_sem("dma_params"))
            for _ in range(SLACK):
                yield
            dve.wait(params)
            dve.done(nc.vector.tensor_scalar(half_gamma[:, :], half_gamma[:, :], 0.5, None, ALU.mult))
            pool.wait(dve.done(nc.vector.tensor_scalar(half_beta[:, :], half_beta[:, :], 0.5, None, ALU.mult)))
            yield

        def chain(*steps):
            for s in steps:
                yield from s

        state = {}
        groups = [(b, g) for g in reversed(range(NT // GROUP)) for b in range(B)]

        def tiles_of(n):
            b, g = groups[n]
            return [b * NT + g * GROUP + i for i in range(GROUP)]

        in_order = [tile for n in range(len(groups)) for tile in tiles_of(n)]
        for e in range(FIRST_PIECES, KD):
            load_piece(wide_b, wq, e)
            load_piece(wide_a, wk, e)
            if e < FIRST_PIECES + len(weight_ring.buffers):
                fetch_block()
        bias_1 = shelf.take()
        load(bias_1, bias_1.ap, gate_b.partition_broadcast(P))
        EARLY, LATE = 3, 2

        gates = gate_tiles(in_order, bias_1)

        second = load_second_fold()

        def folded_tile(source, stored):
            return lambda k: fetch_feature_tile(source, k, stored)

        def chain_start(steps):
            next(steps)
            yield

        def stage_1():
            yield from alongside(first_fold, chain(split_gate(), chain_start(second), part(gates, 1)),
                                 FOLD_SPLIT_PACE)
            yield from alongside(part(gates, EARLY), second, GATE_FETCH_PACE)
            yield from alongside(fold(wide_b, wide_a, vo_dram, vo_stored, "vo"),
                                 chain(save_gate_pair(), fetch_params()), FOLD_SAVE_PACE)
            yield from alongside(part(gates, len(in_order) - EARLY - LATE),
                                 chain(split_weights("qk", wide_a, folded_tile(qk_dram, qk_stored), 2),
                                       split_weights("vo", wide_b, folded_tile(vo_dram, vo_stored), 2)),
                                 GATE_SPLIT_PACE)

        run(alongside(stage_1(), think_1, PACE_1))
        publish_thought()

        x1_stored, x2_stored = {}, {}

        def end_ffn_pool(xb, gb, hb, batch):
            pool.wait(gb.ready, thought_row.ready)
            t = pool.done(nc.gpsimd.tensor_tensor(gb.ap, gb.ap, thought_row.ap[:, batch, :], ALU.mult))
            gb.ready = thought_row.free = [t]
            pool.wait(xb.ready, hb.ready)
            xb.ready = [pool.done(nc.gpsimd.tensor_tensor(xb.ap, xb.ap, half_beta[:, :], ALU.add))]

        def end_ffn_sum(gb, hb):
            dve.wait(gb.ready, hb.ready, hb.free)
            gb.free = [dve.done(nc.vector.tensor_tensor(hb.ap, hb.ap, gb.ap, ALU.add))]
            st = moments(hb.ap, EPS_FFN)
            return st, one_over_std(st, st.ap[:, 4:5])

        def end_ffn_norm(xb, hb, st, t):
            dve.done(nc.vector.scalar_tensor_tensor(out=hb.ap, in0=hb.ap, scalar=st.ap[:, 0:1],
                                                    in1=half_gamma[:, :], op0=ALU.subtract, op1=ALU.mult))
            dve.wait(t, xb.ready)
            t = dve.done(nc.vector.scalar_tensor_tensor(
                out=xb.ap, in0=hb.ap, scalar=st.ap[:, 4:5], in1=xb.ap, op0=ALU.mult, op1=ALU.add))
            xb.ready, hb.free, st.free = [t], [t], [t]

        def fetch_group(n):
            for tile in tiles_of(n):
                state["xg", tile] = fetch(tile, x_flat), fetch(tile, gate1_dram, gate_stored[tile])

        def prepare_group(n):
            made = []
            for tile in tiles_of(n):
                xb, gb = state.pop(("xg", tile))
                hb = shelf.take()
                act.wait(xb.ready, hb.free)
                t = act.done(nc.scalar.activation(hb.ap, xb.ap, ACT.Identity,
                                                  bias=token_stats[:, tile, 1:2],
                                                  scale=token_stats[:, tile, 0:1]))
                hb.ready, hb.free = [t], []
                end_ffn_pool(xb, gb, hb, groups[n][0])
                yield
                yield
                end_ffn_norm(xb, hb, *end_ffn_sum(gb, hb))
                shelf.give(gb)
                yield
                x1_stored[tile] = store(xb, x1_dram[row_of(tile), :], xb.ap)
                dve.wait(xb.ready)
                st = stat_ring.take()
                pool.wait(st.free)
                t = normalisers(xb.ap, st.ap[:, 5:7], EPS_OUTER)
                for _ in range(3):
                    yield
                act.wait(t, hb.free)
                t = act.done(nc.scalar.activation(hb.ap, xb.ap, ACT.Identity,
                                                  bias=st.ap[:, 6:7], scale=st.ap[:, 5:6]))
                st.free = [t]
                hb.ready, hb.free = [t], []
                xb.free.append(t)
                shelf.give(xb)
                made.append(hb)
                yield
            state["h", n] = made

        def turn_group(n):
            pair = group_ring.take()
            halves = pair.ap.rearrange("p a d -> p (a d)").bitcast(F16).rearrange(
                "p (h k t) -> p h k t", h=2, k=KD)
            for i, h in enumerate(state.pop(("h", n))):
                at = slice(i * P, (i + 1) * P)
                for t in turn_tile(h, halves[:, 0, :, at], halves[:, 1, :, at], pair.free):
                    yield
                shelf.give(h)
                yield
            pair.ready, pair.free = [t], []
            state["group", n] = pair, halves

        high_qk, low_qk = halves_of(wide_a)
        high_vo, low_vo = halves_of(wide_b)

        def side_by_side(bufs):
            low, high = bufs[0].slot, bufs[-1].slot
            return halves_in_arena[:, low:high + 1:max(high - low, 1)]

        def queries_and_values(n):
            group, group_halves = state["group", n]
            q = sorted((query_shelf.take() for _ in range(GROUP)), key=lambda buf: buf.slot)
            q_halves = side_by_side(q)
            per_bank = BANK // (GROUP * P)
            for e0 in range(0, KD, per_bank):
                bank = product_ring.take()
                pe.wait(group.ready, wide_a.ready, bank.free)
                for e in range(e0, e0 + per_bank):
                    cols = slice(e * P, (e + 1) * P)
                    for t in pair_product(
                            bank.ap[:, (e - e0) * GROUP * P:(e - e0 + 1) * GROUP * P],
                            (lambda k: high_qk[:, k, cols], lambda k: low_qk[:, k, cols]),
                            (lambda k: group_halves[:, 0, k, :], lambda k: group_halves[:, 1, k, :])):
                        pass
                    yield
                made = bank.ap.rearrange("p (e g t) -> p g e t", e=per_bank, g=GROUP)
                act.wait(t, *(buf.free for buf in q))
                high, low = ([q_halves[:, i, half, e0:e0 + per_bank, :] for i in range(GROUP)]
                             for half in range(2))
                for i in range(GROUP):
                    t2 = act.done(nc.scalar.activation(high[i], made[:, i], ACT.Copy, scale=QUERY_SCALE))
                dve.wait(t2)
                for i in range(GROUP):
                    t2 = dve.done(nc.vector.scalar_tensor_tensor(
                        out=low[i], in0=made[:, i], scalar=QUERY_SCALE, in1=high[i],
                        op0=ALU.mult, op1=ALU.subtract))
                bank.free = [t2]
            wide_a.free = [t]
            for buf in q:
                buf.ready, buf.free = [t2], []
            v = [shelf.take() for _ in range(GROUP)]
            for i in range(GROUP):
                at = slice(i * P, (i + 1) * P)
                for h in range(HALVES):
                    bank = product_ring.take()
                    cols = slice(h * BANK, (h + 1) * BANK)
                    pe.wait(wide_b.ready, bank.free)
                    for t in pair_product(bank.ap,
                                          (lambda k: group_halves[:, 0, k, at], lambda k: group_halves[:, 1, k, at]),
                                          (lambda k: high_vo[:, k, cols], lambda k: low_vo[:, k, cols])):
                        yield
                    act.wait(t, v[i].free)
                    t2 = act.done(nc.scalar.activation(v[i].ap[:, cols], bank.ap, ACT.Copy,
                                                       scale=inverse["vo"][:, :]))
                    bank.free = [t2]
                v[i].ready, v[i].free = [t2], []
            group.free = [t]
            state["qv", n] = (q, v)

        def score(n, i, queries):
            group, group_halves = state["group", n]
            queries = sorted(queries, key=lambda query: query[0].slot)
            q_halves = side_by_side([query[0] for query in queries])
            count = len(queries)
            keys = slice(i * P, (i + 1) * P)
            bank = product_ring.take()
            pe.wait(group.ready, bank.free, *(q.ready for q, _, _, _ in queries))
            out = bank.ap[:, 0:count * P].rearrange("p (g t) -> p g t", t=P)
            for t in pair_product(out, (lambda k: group_halves[:, 0, k, keys], lambda k: group_halves[:, 1, k, keys]),
                                  (lambda k: q_halves[:, :, 0, k, :], lambda k: q_halves[:, :, 1, k, :])):
                yield
            group.free = [t]
            dve.wait(t)
            for at, (q, w, side, keep) in enumerate(queries):
                q.free = [t]
                dve.wait(w.free)
                dve.done(nc.vector.scalar_tensor_tensor(
                    out=w.ap[:, side, :], in0=bank.ap[:, at * P:(at + 1) * P], scalar=score_scale[:, :],
                    in1=keep[:, :], op0=ALU.mult, op1=ALU.min))
                w.ready = [dve.done(nc.vector.scalar_tensor_tensor(
                    out=w.ap[:, side, :], in0=w.ap[:, side, :], scalar=0.0, in1=w.ap[:, side, :],
                    op0=ALU.max, op1=ALU.mult))]
            bank.free = list(w.ready)

        def collect(tile, w, values):
            x2 = state.pop(("x1", tile))
            for h in range(HALVES):
                cols = slice(h * BANK, (h + 1) * BANK)
                bank = product_ring.take()
                pe.wait(w.ready, bank.free)
                for side, v in enumerate(values):
                    pe.wait(v.ready)
                    mm = nc.tensor.matmul(bank.ap, w.ap[:, side, :], v.ap[:, cols],
                                          start=(side == 0), stop=(side == len(values) - 1))
                t = pe.done(mm)
                dve.wait(t, x2.ready)
                t2 = dve.done(nc.vector.tensor_tensor(x2.ap[:, cols], bank.ap, x2.ap[:, cols], ALU.add))
                bank.free = [t2]
                yield
            w.free = [t]
            for v in values:
                v.free.append(t)
            x2.ready = [t2]
            x2_stored[tile] = store(x2, x2_dram[row_of(tile), :], x2.ap)
            shelf.give(x2)

        def attention(n):
            waiting = state.setdefault("waiting", {})
            b, g = groups[n]
            (q0, q1), (v0, v1) = state.pop(("qv", n))
            t0, t1 = tiles_of(n)
            w0, w1 = key_weights.take(), key_weights.take()
            after = waiting.pop(b, None)
            for tile in ([after[0]] if after else []) + [t1] + ([t0] if g == 0 else []):
                state["x1", tile] = fetch(tile, x1_dram, x1_stored[tile])
            yield from score(n, 1, [(q1, w1, 0, keep_own)] + ([(after[1], after[2], 1, keep_prev)] if after else []))
            yield from score(n, 0, [(q0, w0, 0, keep_own), (q1, w1, 1, keep_prev)])
            query_shelf.give(q1)
            if after:
                tile, q, w, v = after
                query_shelf.give(q)
                yield from collect(tile, w, (v, v1))
                shelf.give(v)
                key_weights.give(w)
            yield from collect(t1, w1, (v1, v0))
            shelf.give(v1)
            key_weights.give(w1)
            if g == 0:
                yield from collect(t0, w0, (v0,))
                shelf.give(v0)
                query_shelf.give(q0)
                key_weights.give(w0)
            else:
                waiting[b] = (t0, q0, w0, v0)
            state.pop(("group", n))

        def stage_2(first, last):
            for n in range(first, last):
                more = n + 1 < len(groups)
                if more:
                    fetch_group(n + 1)
                yield from alongside(queries_and_values(n), prepare_group(n + 1) if more else iter(()),
                                     VALUES_GROUP_PACE)
                yield from alongside(attention(n), turn_group(n + 1) if more else prepare_stage_3(),
                                     ATTENTION_TURN_PACE)

        order_3 = sorted(range(B * NT), key=lambda tile: in_order.index(tile) + 5 * (tile % GROUP == 0))
        fetched, measured, prepared, pairs_3, gates_3, sums_3 = {}, {}, {}, {}, {}, {}

        def fetch_3(n):
            if n < len(order_3):
                fetched[n] = fetch(order_3[n], x2_dram, x2_stored[order_3[n]])

        def measure_3(n):
            if n < len(order_3):
                xb = fetched[n]
                dve.wait(xb.ready)
                measured[n] = normalisers(xb.ap, token_stats[:, order_3[n], :], EPS_OUTER)

        def prepare_3(n):
            if n < len(order_3):
                xb, hb = fetched.pop(n), shelf.take()
                stats = token_stats[:, order_3[n], :]
                act.wait(measured[n], xb.ready, hb.free)
                t = act.done(nc.scalar.activation(hb.ap, xb.ap, ACT.Identity,
                                                  bias=stats[:, 1:2], scale=stats[:, 0:1]))
                hb.ready, hb.free = [t], []
                prepared[n] = xb, hb

        def turn_3(n):
            if n < len(order_3):
                yield from turn_and_split(prepared[n][1])
                pairs_3[n] = state["pair"]

        def prepare_stage_3():
            load(wide_a, wide_a.ap.rearrange("p k d -> p (k d)"), gate_pair_dram, gate_pair.saved)
            bias = state["bias"] = shelf.take()
            load(bias, bias.ap, gate_b.partition_broadcast(P))
            for n in range(4):
                fetch_3(n)
            for n in range(3):
                measure_3(n)
                yield
            for n in range(2):
                prepare_3(n)
                yield
            yield from turn_3(0)

        def sum_3(n):
            if 0 <= n < len(order_3):
                gate = gates_3.pop(n)
                sums_3[n] = end_ffn_sum(gate, prepared[n][1])
                shelf.give(gate)

        def end_3(n):
            if 0 <= n < len(order_3):
                xb, hb = prepared.pop(n)
                end_ffn_norm(xb, hb, *sums_3.pop(n))
                shelf.give(hb)
                store(xb, out_flat[row_of(order_3[n]), :], xb.ap)
                shelf.give(xb)

        def gated_3(n):
            if 0 <= n < len(order_3):
                xb, hb = prepared[n]
                end_ffn_pool(xb, gates_3[n], hb, order_3[n] // NT)

        def stage_3():
            for n in range(len(order_3)):
                sum_3(n - 2)
                yield from turn_3(n + 1)
                fetch_3(n + 4)
                gated_3(n - 1)
                prepare_3(n + 2)
                measure_3(n + 3)
                yield from gate_product(pairs_3.pop(n), wide_a, wide_a.ready, state["bias"],
                                        lambda: end_3(n - 2))
                gates_3[n] = state["gate"]
            n = len(order_3)
            gated_3(n - 1)
            for tile in (n - 2, n - 1):
                sum_3(tile)
                end_3(tile)

        fetch_group(0)
        run(alongside(part(gates, LATE), prepare_group(0), GATE_GROUP_PACE))
        run(gates)
        shelf.give(bias_1)
        dve.wait(wide_a.ready)
        act.wait(dve.done(nc.vector.tensor_scalar(score_scale[:, :], inverse["qk"][:, :],
                                                  1.0 / (QUERY_SCALE * TOKEN_SCALE * P), None, ALU.mult)))
        for i in range(KD):
            buf = tile_buffer(i)
            buf.free = gate_pair.free + [gate_pair.saved]
            (query_shelf if i < QUERY_TILES else shelf).give(buf)
        run(turn_group(0))
        run(stage_2(0, B))
        last_tiles = [b * NT + NT - 1 for b in range(B)]
        think_2 = think(lambda b: x2_dram[(b + 1) * T - 1, :].rearrange("(k p) -> k p", p=P),
                        [x2_stored[t] for t in last_tiles])
        run(alongside(stage_2(B, len(groups)), think_2, PACE_2))
        publish_thought()
        shelf.give(*query_shelf.free)
        run(stage_3())
        issue_stores(lambda s: True)
        sp.wait(*(Ticket(sem, n) for sem, n in dma_sems.values() if n))


_INS = ['x', 'w_attn', 'w_o', 'in_gamma', 'in_beta', 'agg_w', 'agg_b', 'pn_gamma', 'pn_beta', 'd1_w', 'd1_b',
        'd2_w', 'd2_b', 'bc_w', 'bc_b', 'gate_w', 'gate_b', 'out_gamma', 'out_beta']


def kernel(**inputs):
    import numpy as _np
    import concourse.bacc as _bacc
    from concourse import mybir as _mybir
    from concourse.bass_utils import run_bass_kernel_spmd as _run

    nc = _bacc.Bacc("TRN2", target_bir_lowering=False, num_devices=1)
    arrays, args = {}, []
    for name in _INS:
        full = ("L0_attn_" if name in ("x", "w_attn", "w_o") else "L0_ffn_") + name
        a = _np.ascontiguousarray(inputs[full])
        arrays[f"in_{name}"] = a
        args.append(nc.dram_tensor(f"in_{name}", a.shape, _mybir.dt.from_np(a.dtype), kind="ExternalInput").ap())
    shape = inputs["L0_attn_x"].shape
    args.append(nc.dram_tensor("out_0", shape, _mybir.dt.float32, kind="ExternalOutput").ap())
    macaron_kernel(nc, *args)
    r = _run(nc, [arrays], core_ids=[0])
    return r.results[0]["out_0"]
```
